# Optimizing a Trainium2 kernel written in Bass

```python
import numpy as np
import jax
import jax.numpy as jnp

def _softmax(x, axis=-1):
    return jax.nn.softmax(x, axis=axis)

def _gelu(x):
    return jax.nn.gelu(x, approximate=True)

def _silu(x):
    return jax.nn.silu(x)

def _sigmoid(x):
    return jax.nn.sigmoid(x)

def _layernorm(x, axis=-1, eps=1e-05):
    m = jnp.mean(x, axis=axis, keepdims=True)
    v = jnp.var(x, axis=axis, keepdims=True)
    return (x - m) / jnp.sqrt(v + eps)

def _scatter_add(tgt, idx, src, axis=0):
    return tgt.at[idx].add(src)

def _segment_sum(src, seg, n):
    return jax.ops.segment_sum(src, seg, n)
kernel_name = 'mk_xattn_ffn_d1_seqx_r8_09ea27'

def setup_inputs(seed: int=0):
    np.random.seed(seed)
    _w = jnp.asarray

    def _rec_inputs():
        import jax
        import jax.numpy as jnp
        _rk = jax.random.key(seed)
        x = 0.0001212 + 1 * jax.random.normal(jax.random.fold_in(_rk, 1), (16, 64, 256), jnp.float32)
        _lenS = 64 - jax.random.randint(jax.random.fold_in(_rk, 7), (16,), 0, max(1, 64 // 4) + 1, jnp.int32)
        _lenS2 = 64 - jax.random.randint(jax.random.fold_in(_rk, 8), (16,), 0, max(1, 64 // 4) + 1, jnp.int32)
        _ctx_2048P = jax.random.normal(jax.random.fold_in(_rk, 11), (16, 16, 256), jnp.float32)
        _ctx_2048c = jax.random.dirichlet(jax.random.fold_in(_rk, 511), 0.3 * jnp.ones((16,), jnp.float32), (16, 64))
        _ctx_2048t = jnp.einsum('bsk,bkd->bsd', _ctx_2048c, _ctx_2048P)
        _ctx_2048t = _ctx_2048t * jax.lax.rsqrt(jnp.mean(jnp.square(_ctx_2048t)) + 1e-12) * 0.953939
        ctx_2048 = 0.000173663 + 1.0001 * (_ctx_2048t + 0.3 * jax.random.normal(jax.random.fold_in(_rk, 611), (16, 64, 256), jnp.float32))
        return (x, ctx_2048)
    x, ctx_2048 = _rec_inputs()

    def _L0_xattn_setup():
        import jax, jax.numpy as jnp
        import numpy as np
        B_DIM, T_DIM, C_DIM = (16, 128, 256)

        def _wkv(w, u, k, v):
            Bn, Tn, Cn = k.shape
            NEG_INF = jnp.float32(-1e+38)

            def step(carry, kv_t):
                p, q, o = carry
                kt, vt = kv_t
                no = jnp.maximum(o, u + kt)
                A = jnp.exp(o - no)
                E = jnp.exp(u + kt - no)
                y = (A * p + E * vt) / (A * q + E)
                no2 = jnp.maximum(w + o, kt)
                A2 = jnp.exp(w + o - no2)
                E2 = jnp.exp(kt - no2)
                return ((A2 * p + E2 * vt, A2 * q + E2, no2), y)
            init = (jnp.zeros((Bn, Cn), k.dtype), jnp.zeros((Bn, Cn), k.dtype), jnp.full((Bn, Cn), NEG_INF, k.dtype))
            kT = jnp.moveaxis(k, 1, 0)
            vT = jnp.moveaxis(v, 1, 0)
            _, yT = jax.lax.scan(step, init, (kT, vT))
            return jnp.moveaxis(yT, 0, 1)
        key = jax.random.key(seed)
        k1, k2, k3, k4 = jax.random.split(key, 4)
        w = -jnp.exp(jax.random.normal(k1, (C_DIM,), jnp.float32))
        u = jax.random.normal(k2, (C_DIM,), jnp.float32)
        k = jax.random.normal(k3, (B_DIM, T_DIM, C_DIM), jnp.float32)
        v = jax.random.normal(k4, (B_DIM, T_DIM, C_DIM), jnp.float32)
        return {'B': B_DIM, 'T': T_DIM, 'C': C_DIM, 'w': w, 'u': u, 'k': k, 'v': v}
    _L0_xattn_all = _L0_xattn_setup()
    _L0_xattn_in = {k: v for k, v in _L0_xattn_all.items() if k in ('w', 'u')}
    del _L0_xattn_all

    def _L0_ffn_setup():
        import jax, jax.numpy as jnp
        import numpy as np
        HIDDEN = 256
        INTER = 96
        N_EXPERTS = 32
        TOP_K = 8
        key = jax.random.key(seed)
        k = jax.random.split(key, 5)
        s = 1.0 / np.sqrt(HIDDEN)
        return {'hidden_states': jax.random.normal(k[0], (1, 128, HIDDEN), jnp.float32), 'gate_w': jax.random.normal(k[1], (HIDDEN, N_EXPERTS), jnp.float32) * s, 'w_gate': jax.random.normal(k[2], (N_EXPERTS, HIDDEN, INTER), jnp.float32) * s, 'w_up': jax.random.normal(k[3], (N_EXPERTS, HIDDEN, INTER), jnp.float32) * s, 'w_down': jax.random.normal(k[4], (N_EXPERTS, INTER, HIDDEN), jnp.float32) * (1.0 / np.sqrt(INTER))}
    _L0_ffn_all = _L0_ffn_setup()
    _L0_ffn_in = {k: v for k, v in _L0_ffn_all.items() if k in ('gate_w', 'w_gate', 'w_up', 'w_down')}
    del _L0_ffn_all
    return {'x': x, 'ctx_2048': ctx_2048, 'L0_xattn_w': _L0_xattn_in['w'], 'L0_xattn_u': _L0_xattn_in['u'], 'L0_ffn_gate_w': _L0_ffn_in['gate_w'], 'L0_ffn_w_gate': _L0_ffn_in['w_gate'], 'L0_ffn_w_up': _L0_ffn_in['w_up'], 'L0_ffn_w_down': _L0_ffn_in['w_down']}

def reference(x, ctx_2048, L0_xattn_w, L0_xattn_u, L0_ffn_gate_w, L0_ffn_w_gate, L0_ffn_w_up, L0_ffn_w_down):
    import jax
    import jax.numpy as jnp

    def _L0_xattn_ref(B, T, C, w, u, k, v):
        import jax, jax.numpy as jnp
        import numpy as np
        B_DIM, T_DIM, C_DIM = (16, 128, 256)

        def _wkv(w, u, k, v):
            Bn, Tn, Cn = k.shape
            NEG_INF = jnp.float32(-1e+38)

            def step(carry, kv_t):
                p, q, o = carry
                kt, vt = kv_t
                no = jnp.maximum(o, u + kt)
                A = jnp.exp(o - no)
                E = jnp.exp(u + kt - no)
                y = (A * p + E * vt) / (A * q + E)
                no2 = jnp.maximum(w + o, kt)
                A2 = jnp.exp(w + o - no2)
                E2 = jnp.exp(kt - no2)
                return ((A2 * p + E2 * vt, A2 * q + E2, no2), y)
            init = (jnp.zeros((Bn, Cn), k.dtype), jnp.zeros((Bn, Cn), k.dtype), jnp.full((Bn, Cn), NEG_INF, k.dtype))
            kT = jnp.moveaxis(k, 1, 0)
            vT = jnp.moveaxis(v, 1, 0)
            _, yT = jax.lax.scan(step, init, (kT, vT))
            return jnp.moveaxis(yT, 0, 1)
        return _wkv(w, u, k, v)

    def _L0_ffn_ref(hidden_states, gate_w, w_gate, w_up, w_down):
        import jax, jax.numpy as jnp
        import numpy as np
        HIDDEN = 256
        INTER = 96
        N_EXPERTS = 32
        TOP_K = 8
        B, S, H = hidden_states.shape
        E = gate_w.shape[1]
        x = hidden_states.reshape(-1, H)
        T = x.shape[0]
        K = TOP_K
        P = T * K
        C = 2 * (P // E)
        probs = jax.nn.softmax(x @ gate_w, axis=-1)
        w, sel = jax.lax.top_k(probs, K)
        w = w / jnp.sum(w, axis=-1, keepdims=True)
        flat_e = sel.reshape(-1)
        flat_t = jnp.repeat(jnp.arange(T), K)
        flat_w = w.reshape(-1)
        order = jnp.argsort(flat_e)
        se = flat_e[order]
        start = jnp.searchsorted(se, jnp.arange(E))
        pos = jnp.arange(P) - start[se]
        slot = jnp.where(pos < C, se * C + pos, E * C)
        slot_pair = jnp.full((E * C,), P, dtype=jnp.int32).at[slot].set(order.astype(jnp.int32), mode='drop')
        t_slot = jnp.concatenate([flat_t, jnp.array([T])])[slot_pair]
        w_slot = jnp.concatenate([flat_w, jnp.zeros((1,), flat_w.dtype)])[slot_pair]
        x_pad = jnp.concatenate([x, jnp.zeros((1, H), x.dtype)], axis=0)
        xg = x_pad[t_slot].reshape(E, C, H)
        g = jnp.einsum('ech,ehi->eci', xg, w_gate)
        u = jnp.einsum('ech,ehi->eci', xg, w_up)
        y = jnp.einsum('eci,eih->ech', jax.nn.silu(g) * u, w_down).reshape(E * C, H)
        out = jnp.zeros((T + 1, H), x.dtype).at[t_slot].add(w_slot[:, None] * y)
        return out[:T].reshape(B, S, H)
    x = x + _L0_xattn_ref(16, 64, 256, L0_xattn_w, L0_xattn_u, _layernorm(x, axis=-1), ctx_2048)
    x = x + _L0_ffn_ref(_layernorm(x, axis=-1), L0_ffn_gate_w, L0_ffn_w_gate, L0_ffn_w_up, L0_ffn_w_down)
    return x

_drawn_inputs = setup_inputs


def setup_inputs(seed=0):
    import zlib

    import numpy as np

    out = dict(_drawn_inputs(seed))
    spreads = {}
    factors = {}
    for name, (base, spread) in spreads.items():
        noise = np.random.default_rng([zlib.crc32(name.encode()), seed]).standard_normal(out[name].shape)
        drawn = base * np.exp(spread * noise) if base else spread * noise
        out[name] = jnp.asarray(drawn.astype(out[name].dtype))
    for name, factor in factors.items():
        out[name] = (out[name] * factor).astype(out[name].dtype)
    return out
```

```python
from contextlib import ExitStack

import concourse.bass as bass
from concourse import mybir

F32 = mybir.dt.float32
F32R = mybir.dt.float32r
BF16 = mybir.dt.bfloat16
ALU = mybir.AluOpType
ACT = mybir.ActivationFunctionType
AX = mybir.AxisListType

P = 128
TOP = 8
EPS = 1e-5
START_MAX = -1e38
RESET = -2e38
NO_WEIGHT = -1e4


class Chain:

    def __init__(self, engine, sem):
        self.engine, self.sem, self.count, self.turn, self.per_turn = engine, sem, 0, None, 0

    def link(self, instruction):
        self.count += 1
        instruction.then_inc(self.sem, 1)
        at = self.count if self.turn is None else self.turn * self.per_turn + self.count
        self.engine.wait_ge(self.sem, at)

    def enter(self, turn, per_turn):
        self.turn, self.per_turn, self.entered = turn, per_turn, self.count

    def leave(self, turns):
        assert self.count - self.entered == self.per_turn, (self.count - self.entered, self.per_turn)
        self.count += (turns - 1) * self.per_turn
        self.turn = None


class Unit:

    def __init__(self, n, tile, tiles, slot, capped, before, looped=False):
        self.n = n
        self.tile = tile
        self.tiles = tiles
        self.slot = slot
        self.capped = capped
        self.before = before
        self.looped = looped


def program(nc, x, ctx_in, decay, bonus, gate_w, w_gate, w_up, w_down, out):
    NB, S, C = x.shape
    E, _, INTER = w_gate.shape
    T = NB * S
    TILES = T // P
    HALF = T // 2
    HT = TILES // 2
    KT = C // P
    BPT = P // S
    NT = 2
    BK = NT * BPT * KT
    SP1 = S + 1
    CAP = 2 * (T * TOP // E)
    FT = E * INTER // P
    EG = 4
    GT = EG * INTER // P
    GF = EG * INTER
    GROUPS = E // EG
    assert GT * P == GF and CAP >= HALF and KT == 2 and GROUPS % 2 == 0
    PART = KT * GF
    assert PART == GT * C

    xt = x.rearrange("b s c -> (b s) c").rearrange("(n p) c -> p n c", p=P)
    ct = ctx_in.rearrange("b s c -> (b s) c").rearrange("(n p) c -> p n c", p=P)
    ot = out.rearrange("b s c -> (b s) c").rearrange("(n p) c -> p n c", p=P)
    wg_dram = w_gate.rearrange("e (p k) i -> p e (k i)", k=KT)
    wu_dram = w_up.rearrange("e (p k) i -> p e (k i)", k=KT)
    wd_dram = w_down.rearrange("e i c -> (e i) c").rearrange("(n p) c -> p n c", p=P)

    with ExitStack() as stack:
        def sb(name, shape, dt=F32):
            return stack.enter_context(nc.sbuf_tensor(name, shape, dt))

        def sem(name):
            return stack.enter_context(nc.semaphore(name))

        ident = sb("ident", [P, P])
        ident_bf = sb("ident_bf", [P, P], BF16)
        ones_bf = sb("ones_bf", [P, P], BF16)
        earlier = sb("earlier", [P, P], BF16)
        zeros_bf = sb("zeros_bf", [P, HALF], BF16)
        expert3 = sb("expert3", [3 * E, E], BF16)
        spread = sb("spread", [3 * E, E, INTER], BF16)
        neg_half = sb("neg_half", [P, HT])
        decay_sb = sb("decay_sb", [P, KT])
        bonus_sb = sb("bonus_sb", [P, KT])
        decays = sb("decays", [P, BK, SP1])
        gate_sb = sb("gate_sb", [P, KT, E])
        gate_hi = sb("gate_hi", [P, KT, E], F32R)
        gate_lo = sb("gate_lo", [P, KT, E], F32R)
        x_sb = sb("x_sb", [P, TILES, C])
        ctx_sb = sb("ctx_sb", [P, TILES, C])
        x1 = sb("x1", [P, TILES, C])
        h_hi = sb("h_hi", [P, KT, T], F32R)
        h_lo = sb("h_lo", [P, KT, T], F32R)
        route = sb("route", [3 * E, T], BF16)
        counts = sb("counts", [P, E])
        def pair(name, shape, dt=F32):
            return [sb(f"{name}{i}", shape, dt) for i in range(2)]

        stats, mv, var, rstd = pair("stats", [P, NT, 6]), pair("mv", [P, NT, 2]), pair("var", [P, NT]), pair("rstd", [P, NT])
        normed = pair("normed", [P, NT, C])
        kpad, vpad, opad = pair("kpad", [P, BK, SP1]), pair("vpad", [P, BK, SP1]), pair("opad", [P, BK, SP1])
        diffs = pair("diffs", [P, 2, BK, S])
        expo = pair("expo", [P, 4, BK, SP1])
        fact = pair("fact", [P, 4, BK, SP1])
        ev2 = pair("ev2", [P, BK, SP1])
        state = pair("state", [P, 2, BK, SP1])
        mixed = pair("mixed", [P, KT * NT * P])
        shifted, expd, replaced = pair("shifted", [P, NT, E]), pair("expd", [P, NT, E]), pair("replaced", [P, NT, E])
        top, top_sum, rowmax = pair("top", [P, NT, TOP]), pair("top_sum", [P, 2, NT]), pair("rowmax", [P, NT])
        mask = pair("mask", [P, NT, E], BF16)
        rank, wts, rest = pair("rank", [P, NT, E]), pair("wts", [P, NT, E]), pair("rest", [P, NT, E])
        parts = pair("parts", [P, NT, 3 * E], BF16)
        raw = [sb(f"raw{i}", [P, 3, PART]) for i in range(2)]
        whi = [sb(f"whi{i}", [P, 3, PART], F32R) for i in range(2)]
        wlo = [sb(f"wlo{i}", [P, 3, PART], F32R) for i in range(2)]
        s_sb = sb("s_sb", [P, HALF])
        t1_sb = sb("t1_sb", [P, HALF])
        t_sb = sb("t_sb", [P, HALF])
        t_hi = [sb(f"t_hi{i}", [P, HALF], F32R) for i in range(2)]
        t_lo = [sb(f"t_lo{i}", [P, HALF], F32R) for i in range(2)]
        y_sb = sb("y_sb", [P, KT, HALF])

        bank = [stack.enter_context(nc.psum_tensor(f"bank{i}", [P, 512], F32)) for i in range(8)]
        y_ps, g_ps, u_ps, w_ps = bank[0:2], bank[2], bank[3], bank[4]
        unit_ps = [(bank[5], bank[6]), (bank[7], bank[4])]

        x_landed = [sem(f"x_landed{i}") for i in range(3)]
        ctx_landed = [sem(f"ctx_landed{i}") for i in range(2)]
        small_landed = sem("small_landed")
        raw_landed = [sem(f"raw_landed{i}") for i in range(2)]
        out_stored = sem("out_stored")
        pool_chain, dve_chain, act_chain = sem("pool_chain"), sem("dve_chain"), sem("act_chain")
        consts_ready, pads_ready, tables_ready = sem("consts_ready"), sem("pads_ready"), sem("tables_ready")
        gate_hi_ready, gate_ready = sem("gate_hi_ready"), sem("gate_ready")
        var_ready, rstd_ready = sem("var_ready"), sem("rstd_ready")
        k_normed, kv_turned, kv_ready = sem("k_normed"), sem("kv_turned"), sem("kv_ready")
        expo_ready, fact_ready, mixed_ready, mixed_turned = sem("expo_ready"), sem("fact_ready"), sem("mixed_ready"), sem("mixed_turned")
        h_normed, h_turned, h_hi_ready, h_lo_ready = sem("h_normed"), sem("h_turned"), sem("h_hi_ready"), sem("h_lo_ready")
        logits_ready, shifted_ready, expd_ready = sem("logits_ready"), sem("shifted_ready"), sem("expd_ready")
        mask_ready, ranks_ready, parts_ready, parts_turned, route_ready = sem("mask_ready"), sem("ranks_ready"), sem("parts_ready"), sem("parts_turned"), sem("route_ready")
        w_hi_ready, w_lo_ready = sem("w_hi_ready"), sem("w_lo_ready")
        w_turned, g_ready, u_ready, down_done = sem("w_turned"), sem("g_ready"), sem("u_ready"), sem("down_done")
        s_ready, t1_ready, t_ready, t_hi_ready, t_lo_ready = sem("s_ready"), sem("t1_ready"), sem("t_ready"), sem("t_hi_ready"), sem("t_lo_ready")
        y_done, y_copied, y_turned, out_ready = sem("y_done"), sem("y_copied"), sem("y_turned"), sem("out_ready")

        units = [Unit(n, NT * n, NT, n % 2, NT * n * P >= HALF, max(n - 1, 0)) for n in range(TILES // NT)]
        half_units = len(units) // 2
        TURNS = GROUPS // 2
        STEPS = GROUPS * GT
        TURN_STEPS = 2 * GT

        def raw_parts(slot, part):
            r = raw[slot][:, part, :]
            if part < 2:
                return r.rearrange("p (e k i) -> p k e i", e=EG, k=KT)
            return r

        def split_view(w, slot, part):
            v = w[slot][:, part, :]
            if part < 2:
                return v.rearrange("p (k e i) -> p k e i", e=EG, k=KT)
            return v

        def up_weight(w, slot, part, k, j):
            at = k * GF + j * P
            return w[slot][:, part, at:at + P]

        def down_weight(w, slot, j, m):
            return w[slot][:, 2, j * C:(j + 1) * C].rearrange("p (c k) -> p k c", k=KT)[:, m, :]

        block = stack.enter_context(nc.Block())

        @block.sync
        def _(sp):
            for u in units[:half_units]:
                sp.dma_start(x_sb[:, u.tile:u.tile + NT, :], xt[:, u.tile:u.tile + NT, :]).then_inc(x_landed[u.n], 16)
            sp.dma_start(x_sb[:, HT:, :], xt[:, HT:, :]).then_inc(x_landed[2], 16)

            def load(slot, group):
                experts = bass.ds(group * EG, EG)
                for part, w in ((0, wg_dram), (1, wu_dram)):
                    sp.dma_start(raw[slot][:, part, :].rearrange("p (e n) -> p e n", e=EG),
                                 w[:, experts, :]).then_inc(raw_landed[slot], 16)
                sp.dma_start(raw[slot][:, 2, :].rearrange("p (n c) -> p n c", n=GT),
                             wd_dram[:, bass.ds(group * GT, GT), :]).then_inc(raw_landed[slot], 16)

            load(0, 0)
            load(1, 1)
            for half in range(2):
                def reload(it):
                    for slot in range(2):
                        done = (half * GROUPS + slot + 1) * 3 + it * 6
                        sp.wait_ge(w_hi_ready, done)
                        sp.wait_ge(w_lo_ready, done)
                        load(slot, it * 2 + 2 + slot)

                with sp.Fori(0, TURNS - 1) as it:
                    reload(it)
                if half == 0:
                    for slot in range(2):
                        done = (GROUPS - 2 + slot + 1) * 3
                        sp.wait_ge(w_hi_ready, done)
                        sp.wait_ge(w_lo_ready, done)
                        load(slot, slot)
            for half in range(2):
                sp.wait_ge(out_ready, half + 1)
                tiles = slice(half * HT, (half + 1) * HT)
                sp.dma_start(ot[:, tiles, :], x1[:, tiles, :]).then_inc(out_stored, 16)
            sp.wait_ge(out_stored, 32)

        @block.gpsimd
        def _(pool):
            chain = Chain(pool, pool_chain)
            pool.memset(ident[:], 0.0)
            pool.memset(ident_bf[:], 0.0)
            pool.memset(expert3[:], 0.0)
            pool.memset(zeros_bf[:], 0.0)
            pool.memset(ones_bf[:], 1.0)
            chain.link(pool.memset(earlier[:], 1.0))
            pool.affine_select(out=ident[:], in_=ident[:], compare_op=ALU.not_equal, fill=1.0, base=0,
                               pattern=[[-1, P]], channel_multiplier=1).then_inc(consts_ready, 1)
            pool.affine_select(out=ident_bf[:], in_=ident_bf[:], compare_op=ALU.not_equal, fill=1.0, base=0,
                               pattern=[[-1, P]], channel_multiplier=1)
            pool.affine_select(out=earlier[:], in_=earlier[:], compare_op=ALU.is_gt, fill=0.0, base=0,
                               pattern=[[1, P]], channel_multiplier=-1)
            for part in range(3):
                chain.link(pool.affine_select(out=expert3[:], in_=expert3[:], compare_op=ALU.not_equal, fill=1.0,
                                              base=-part * E, pattern=[[-1, E]], channel_multiplier=1))
            pool.memset(neg_half[:], -0.5).then_inc(consts_ready, 1)

            def split_low(slot, part, group):
                pool.wait_ge(w_hi_ready, group * 3 + part + 1)
                if not isinstance(group, int) or group >= 2:
                    pool.wait_ge(down_done, (group - 1) * GT + 1)
                pool.tensor_tensor(split_view(wlo, slot, part), raw_parts(slot, part),
                                   split_view(whi, slot, part).bitcast(F32), ALU.subtract).then_inc(w_lo_ready, 1)

            pool.wait_ge(consts_ready, 2)
            for pair_at in range(0, len(units), 2):
                for which in range(2):
                    for u in units[pair_at:pair_at + 2]:
                        pool.wait_ge(var_ready, 2 * pair_at + 2 * which + (u.n - pair_at) + 1)
                        n = slice(0, u.tiles)
                        pool.tensor_tensor(rstd[u.slot][:, n], var[u.slot][:, n], neg_half[:, n], ALU.pow).then_inc(rstd_ready, 1)
                if pair_at == 0:
                    for part in range(3):
                        split_low(0, part, 0)
            for half in range(2):
                base = half * GROUPS
                with pool.Fori(0, TURNS - 1) as it:
                    for ahead in (1, 2):
                        for part in range(3):
                            split_low(ahead % 2, part, it * 2 + (base + ahead))
                last = base + GROUPS - 2
                for ahead in (1, 2) if half == 0 else (1,):
                    for part in range(3):
                        split_low(ahead % 2, part, last + ahead)

        @block.scalar
        def _(act):
            act.dma_start(ctx_sb[:, 0:HT, :], ct[:, 0:HT, :]).then_inc(ctx_landed[0], 16)
            act.dma_start(decay_sb[:], decay.rearrange("(p k) -> p k", k=KT)).then_inc(small_landed, 16)
            act.dma_start(bonus_sb[:], bonus.rearrange("(p k) -> p k", k=KT)).then_inc(small_landed, 16)
            act.dma_start(gate_sb[:], gate_w.rearrange("(p k) e -> p k e", k=KT)).then_inc(small_landed, 16)
            act.dma_start(ctx_sb[:, HT:, :], ct[:, HT:, :]).then_inc(ctx_landed[1], 16)
            act.wait_ge(small_landed, 48)
            nc.scalar.activation(gate_hi[:], gate_sb[:], ACT.Copy).then_inc(gate_hi_ready, 1)

            def take_kv(u):
                act.wait_ge(kv_turned, u.n + 1)
                bk = u.tiles * BPT * KT
                for ps, pad in zip(unit_ps[u.slot], (kpad, vpad)):
                    to = pad[u.slot][:, 0:bk, 1:].rearrange("p (b k) s -> p k b s", k=KT)
                    fr = ps[:, 0:KT * u.tiles * P].rearrange("p (k b s) -> p k b s", k=KT, s=S)
                    last = nc.scalar.activation(to, fr, ACT.Copy)
                last.then_inc(kv_ready, 1)

            def exps(u):
                act.wait_ge(expo_ready, u.n + 1)
                bk = u.tiles * BPT * KT
                nc.scalar.activation(fact[u.slot][:, :, 0:bk, :], expo[u.slot][:, :, 0:bk, :], ACT.Exp).then_inc(fact_ready, 1)

            def take_h(u):
                act.wait_ge(h_turned, u.n + 1)
                cols = u.tiles * P
                fr = unit_ps[u.slot][1][:, 0:KT * cols].rearrange("p (k t) -> p k t", k=KT)
                at = u.tile * P
                nc.scalar.activation(h_hi[:, :, at:at + cols], fr, ACT.Copy).then_inc(h_hi_ready, 1)

            def route_exps(u):
                act.wait_ge(shifted_ready, u.n + 1)
                n = slice(0, u.tiles)
                nc.scalar.activation(expd[u.slot][:, n, :], shifted[u.slot][:, n, :], ACT.Exp).then_inc(expd_ready, 1)

            def take_route(u):
                act.wait_ge(parts_turned, u.n + 1)
                cols = u.tiles * P
                at = u.tile * P
                fr = unit_ps[u.slot][0][:].bitcast(BF16)[0:3 * E, 0:cols]
                nc.scalar.activation(route[:, at:at + cols], fr, ACT.Copy).then_inc(route_ready, 1)

            def split_high(slot, part, group):
                act.wait_ge(raw_landed[slot], group * 24 + (48 - slot * 24))
                if not isinstance(group, int) or group >= 2:
                    act.wait_ge(down_done, (group - 1) * GT + 1)
                nc.scalar.activation(split_view(whi, slot, part), raw_parts(slot, part), ACT.Copy).then_inc(w_hi_ready, 1)

            for pair_at in range(0, len(units), 2):
                for stage in (take_kv, exps, take_h, route_exps, take_route):
                    for u in units[pair_at:pair_at + 2]:
                        stage(u)
                    if pair_at == 0 and stage is take_kv:
                        for part in range(3):
                            split_high(0, part, 0)

            def step(n, k):
                act.wait_ge(g_ready, n + 1)
                act.wait_ge(t1_ready, n)
                nc.scalar.activation(s_sb[:], g_ps[:], ACT.Silu).then_inc(s_ready, 1)
                act.wait_ge(t_ready, n + 1)
                act.wait_ge(down_done, n)
                nc.scalar.activation(t_hi[k % 2][:], t_sb[:], ACT.Copy).then_inc(t_hi_ready, 1)

            for half in range(2):
                def turn(it, last):
                    for k in range(TURN_STEPS):
                        step(it * TURN_STEPS + (half * STEPS + k), k)
                        ahead = k // GT + 1
                        if not (last and ahead == 2):
                            split_high(ahead % 2, k % GT, it * 2 + (half * GROUPS + ahead))

                with act.Fori(0, TURNS - 1) as it:
                    turn(it, False)
                turn(TURNS - 1, half == 1)
                act.wait_ge(y_done, half + 1)
                if half:
                    act.wait_ge(y_turned, half)
                nc.scalar.activation(y_sb[:, 0, :], y_ps[0][:], ACT.Copy).then_inc(y_copied, 1)

        @block.tensor
        def _(pe):
            def turn_kv(u):
                if u.n == 0:
                    pe.wait_ge(consts_ready, 1)
                pe.wait_ge(k_normed, u.n + 1)
                pe.wait_ge(ctx_landed[1 if u.capped else 0], 16)
                if u.before:
                    pe.wait_ge(route_ready, u.before)
                for ps, src in zip(unit_ps[u.slot], (normed[u.slot], ctx_sb[:, u.tile:u.tile + u.tiles, :])):
                    for t in range(u.tiles):
                        rows = src[:, t, :].rearrange("p (c k) -> p k c", k=KT)
                        for k in range(KT):
                            at = (k * u.tiles + t) * P
                            last = nc.tensor.transpose(ps[:, at:at + P], rows[:, k, :], ident[:])
                last.then_inc(kv_turned, 1)

            def turn_mixed(u):
                pe.wait_ge(mixed_ready, u.n + 1)
                for t in range(u.tiles):
                    for k in range(KT):
                        at = (t * KT + k) * P
                        last = nc.tensor.transpose(unit_ps[u.slot][0][:, at:at + P], 
                                                   mixed[u.slot][:, (k * u.tiles + t) * P:(k * u.tiles + t + 1) * P], ident[:])
                last.then_inc(mixed_turned, 1)

            def turn_h(u):
                pe.wait_ge(h_normed, u.n + 1)
                for t in range(u.tiles):
                    rows = normed[u.slot][:, t, :].rearrange("p (c k) -> p k c", k=KT)
                    for k in range(KT):
                        at = (k * u.tiles + t) * P
                        last = nc.tensor.transpose(unit_ps[u.slot][1][:, at:at + P], rows[:, k, :], ident[:])
                last.then_inc(h_turned, 1)

            def logits(u):
                pe.wait_ge(h_hi_ready, u.n + 1)
                pe.wait_ge(h_lo_ready, u.n + 1)
                if u.n == 0:
                    pe.wait_ge(gate_ready, 1)
                for t in range(u.tiles):
                    cols = slice((u.tile + t) * P, (u.tile + t + 1) * P)
                    terms = [(a, b, k) for k in range(KT) for a, b in ((h_hi, gate_hi), (h_hi, gate_lo), (h_lo, gate_hi))]
                    for n, (a, b, k) in enumerate(terms):
                        last = nc.tensor.matmul(unit_ps[u.slot][0][:, t * E:(t + 1) * E], a[:, k, cols], b[:, k, :],
                                                start=(n == 0), stop=(n == len(terms) - 1))
                last.then_inc(logits_ready, 1)

            def ranks(u):
                pe.wait_ge(mask_ready, u.n + 1)
                if u.n == 0:
                    pe.wait_ge(consts_ready, 2)
                ps = unit_ps[u.slot][1]
                if u.capped:
                    for t in range(u.tiles):
                        for s in range(t + 1):
                            nc.tensor.matmul(ps[:, t * E:(t + 1) * E], (earlier if s == t else ones_bf)[:], mask[u.slot][:, s, :],
                                             start=(s == 0), stop=(s == t))
                for s in range(u.tiles):
                    last = nc.tensor.matmul(ps[:, NT * E:(NT + 1) * E], ones_bf[:], mask[u.slot][:, s, :],
                                            start=(s == 0), stop=(s == u.tiles - 1))
                last.then_inc(ranks_ready, 1)

            def turn_parts(u):
                pe.wait_ge(parts_ready, u.n + 1)
                to = unit_ps[u.slot][0][:].bitcast(BF16)
                for t in range(u.tiles):
                    last = nc.tensor.transpose(to[0:3 * E, t * P:(t + 1) * P], parts[u.slot][:, t, :], ident_bf[:])
                last.then_inc(parts_turned, 1)

            for pair_at in range(0, len(units), 2):
                for stage in (turn_kv, turn_mixed, turn_h, logits, ranks, turn_parts):
                    for u in units[pair_at:pair_at + 2]:
                        stage(u)

            def up(n, half, slot, j, tile):
                tokens = slice(half * HALF, (half + 1) * HALF)
                pe.wait_ge(t1_ready, n)
                nc.tensor.matmul(w_ps[:], spread[:].rearrange("p e i -> p (e i)")[:, bass.ds(tile * P, P)],
                                 route[:, tokens], start=True, stop=True).then_inc(w_turned, 1)
                pe.wait_ge(s_ready, n)
                for part, ps, ready in ((0, g_ps, g_ready), (1, u_ps, u_ready)):
                    if part == 1:
                        pe.wait_ge(t_ready, n)
                    terms = [(w, h, k) for k in range(KT) for w, h in ((whi, h_hi), (whi, h_lo), (wlo, h_hi))]
                    for i, (w, h, k) in enumerate(terms):
                        last = nc.tensor.matmul(ps[:], up_weight(w, slot, part, k, j), h[:, k, tokens],
                                                start=(i == 0), stop=(i == len(terms) - 1))
                    last.then_inc(ready, 1)

            def down(n, slot, j, odd):
                pe.wait_ge(t_hi_ready, n + 1)
                for m in range(KT):
                    nc.tensor.matmul(y_ps[m][:], down_weight(whi, slot, j, m), t_hi[odd][:], start=False, stop=False)
                    nc.tensor.matmul(y_ps[m][:], down_weight(wlo, slot, j, m), t_hi[odd][:], start=False, stop=False)
                pe.wait_ge(t_lo_ready, n + 1)
                for m in range(KT):
                    last = nc.tensor.matmul(y_ps[m][:], down_weight(whi, slot, j, m), t_lo[odd][:], start=False, stop=False)
                last.then_inc(down_done, 1)

            for half in range(2):
                pe.wait_ge(route_ready, half_units * (half + 1))
                if half == 0:
                    pe.wait_ge(tables_ready, 1)
                else:
                    pe.wait_ge(y_copied, 2 * half)
                for m in range(KT):
                    first = nc.tensor.matmul(y_ps[m][:], zeros_bf[:, 0:P], zeros_bf[:], start=True, stop=False)
                if half == 0:
                    first.then_inc(down_done, 1)

                def turn(it, first_turn):
                    for k in range(TURN_STEPS):
                        n = it * TURN_STEPS + (half * STEPS + k)
                        slot, j = k // GT, k % GT
                        if j == 0:
                            group = it * 2 + (half * GROUPS + slot)
                            pe.wait_ge(w_hi_ready, group * 3 + 3)
                            pe.wait_ge(w_lo_ready, group * 3 + 3)
                        up(n, half, slot, j, it * TURN_STEPS + k)
                        if k > 0:
                            down(n - 1, (k - 1) // GT, (k - 1) % GT, (k - 1) % 2)
                        elif not first_turn:
                            down(n - 1, 1, GT - 1, 1)

                turn(0, True)
                with pe.Fori(1, TURNS) as it:
                    turn(it, False)
                down(half * STEPS + STEPS - 1, 1, GT - 1, 1)
                for m in range(KT):
                    last = nc.tensor.matmul(y_ps[m][:], zeros_bf[:, 0:P], zeros_bf[:], start=False, stop=True)
                last.then_inc(y_done, 1)
                pe.wait_ge(y_copied, 2 * (half + 1))
                if half:
                    pe.wait_ge(out_ready, half)
                for t in range(HT):
                    ps = unit_ps[0][t // 2]
                    for k in range(KT):
                        at = ((t % 2) * KT + k) * P
                        last = nc.tensor.transpose(ps[:, at:at + P], y_sb[:, k, t * P:(t + 1) * P], ident[:])
                last.then_inc(y_turned, 1)

        @block.vector
        def _(dve):
            chain = Chain(dve, dve_chain)
            link = chain.link
            for s in range(2):
                nc.vector.memset(kpad[s][:, :, 0:1], START_MAX)
                nc.vector.memset(vpad[s][:, :, 0:1], 0.0)
                for q in range(4):
                    nc.vector.memset(expo[s][:, q, :, 0:1], NO_WEIGHT)
            nc.vector.memset(counts[:], 0.0)
            link(nc.vector.memset(decays[:], 0.0))

            def norm_stats(u, src):
                for t in range(u.tiles):
                    nc.vector.bn_stats(stats[u.slot][:, t, :], src[:, u.tile + t, :])
                link(nc.vector.memset(top_sum[u.slot][:, 1, :], 0.0))
                for t in range(u.tiles):
                    last = nc.vector.bn_aggr(mv[u.slot][:, t, :], stats[u.slot][:, t, :])
                link(last)
                n = slice(0, u.tiles)
                nc.vector.tensor_scalar(var[u.slot][:, n], mv[u.slot][:, n, 1], EPS, None, ALU.add).then_inc(var_ready, 1)

            def norm_apply(u, src, ready, order):
                dve.wait_ge(rstd_ready, order)
                for t in range(u.tiles):
                    last = nc.vector.tensor_scalar(normed[u.slot][:, t, :], src[:, u.tile + t, :], mv[u.slot][:, t, 0:1],
                                                   rstd[u.slot][:, t:t + 1], ALU.subtract, ALU.mult)
                last.then_inc(ready, 1)

            def stats_x(u):
                dve.wait_ge(x_landed[min(u.n, 2)], 16)
                if u.before:
                    dve.wait_ge(route_ready, u.before)
                norm_stats(u, x_sb)

            def norm_x(u):
                norm_apply(u, x_sb, k_normed, 4 * (u.n // 2) + u.n % 2 + 1)

            def tables(u):
                if u.n:
                    return
                dve.wait_ge(small_landed, 48)
                dve.wait_ge(gate_hi_ready, 1)
                nc.vector.tensor_tensor(gate_lo[:], gate_sb[:], gate_hi[:].bitcast(F32), ALU.subtract).then_inc(gate_ready, 1)
                by = decays[:].rearrange("p (b k) s -> p b k s", k=KT)
                for k in range(KT):
                    nc.vector.tensor_scalar(by[:, :, k, 1:], by[:, :, k, 1:], decay_sb[:, k:k + 1], None, ALU.add)
                link(nc.vector.memset(decays[:, :, 0:1], RESET))

            def exponents(u):
                dve.wait_ge(kv_ready, u.n + 1)
                bk = u.tiles * BPT * KT
                k_, o_ = kpad[u.slot], opad[u.slot]
                flat = lambda a: a[:, 0:bk, :].rearrange("p b s -> p (b s)")
                link(nc.vector.tensor_tensor_scan(flat(o_), flat(decays), flat(k_), 0.0, ALU.add, ALU.max))
                for k in range(KT):
                    now = k_[:, 0:bk, :].rearrange("p (b k) s -> p b k s", k=KT)[:, :, k, 1:]
                    was = o_[:, 0:bk, :].rearrange("p (b k) s -> p b k s", k=KT)[:, :, k, 0:S]
                    d = diffs[u.slot][:, :, 0:bk, :].rearrange("p q (b k) s -> p q b k s", k=KT)
                    nc.vector.scalar_tensor_tensor(out=d[:, 0, :, k, :], in0=now, scalar=bonus_sb[:, k:k + 1], in1=was,
                                                   op0=ALU.add, op1=ALU.subtract)
                    last = nc.vector.scalar_tensor_tensor(out=d[:, 1, :, k, :], in0=was, scalar=decay_sb[:, k:k + 1], in1=now,
                                                          op0=ALU.add, op1=ALU.subtract)
                link(last)
                nc.vector.tensor_scalar(expo[u.slot][:, 0:2, 0:bk, 1:], diffs[u.slot][:, :, 0:bk, :], 0.0, None, ALU.min)
                nc.vector.tensor_scalar(expo[u.slot][:, 2:4, 0:bk, 1:], diffs[u.slot][:, :, 0:bk, :], -1.0, 0.0,
                                        ALU.mult, ALU.min).then_inc(expo_ready, 1)

            def mix(u):
                dve.wait_ge(fact_ready, u.n + 1)
                bk = u.tiles * BPT * KT
                f, st = fact[u.slot], state[u.slot]
                flat = lambda a: a.rearrange("p b s -> p (b s)")
                e, a2, a, e2 = (f[:, q, 0:bk, :] for q in range(4))
                link(nc.vector.tensor_tensor(ev2[u.slot][:, 0:bk, :], e2, vpad[u.slot][:, 0:bk, :], ALU.mult))
                nc.vector.tensor_tensor_scan(flat(st[:, 0, 0:bk, :]), flat(a2), flat(ev2[u.slot][:, 0:bk, :]), 0.0, ALU.mult, ALU.add)
                link(nc.vector.tensor_tensor_scan(flat(st[:, 1, 0:bk, :]), flat(a2), flat(e2), 0.0, ALU.mult, ALU.add))
                num, den = (diffs[u.slot][:, q, 0:bk, :] for q in range(2))
                ev = opad[u.slot][:, 0:bk, 1:]
                nc.vector.tensor_tensor(ev, e[:, :, 1:], vpad[u.slot][:, 0:bk, 1:], ALU.mult)
                nc.vector.tensor_tensor(num, a[:, :, 1:], st[:, 0, 0:bk, 0:S], ALU.mult)
                link(nc.vector.tensor_tensor(den, a[:, :, 1:], st[:, 1, 0:bk, 0:S], ALU.mult))
                nc.vector.tensor_tensor(num, num, ev, ALU.add)
                link(nc.vector.tensor_tensor(den, den, e[:, :, 1:], ALU.add))
                link(nc.vector.reciprocal(den, den))
                by_token = lambda v: v.rearrange("p (b k) s -> p b k s", k=KT)
                y = mixed[u.slot][:, 0:bk * S].rearrange("p (k b s) -> p b k s", k=KT, s=S)
                nc.vector.tensor_tensor(y, by_token(num), by_token(den), ALU.mult).then_inc(mixed_ready, 1)

            def add_mixed(u):
                dve.wait_ge(mixed_turned, u.n + 1)
                for t in range(u.tiles):
                    y = unit_ps[u.slot][0][:, t * C:(t + 1) * C].rearrange("p (k c) -> p c k", k=KT)
                    last = nc.vector.tensor_tensor(x1[:, u.tile + t, :].rearrange("p (c k) -> p c k", k=KT),
                                                   x_sb[:, u.tile + t, :].rearrange("p (c k) -> p c k", k=KT), y, ALU.add)
                link(last)
                norm_stats(u, x1)

            def norm_h(u):
                norm_apply(u, x1, h_normed, 4 * (u.n // 2) + 2 + u.n % 2 + 1)

            def h_low(u):
                dve.wait_ge(h_hi_ready, u.n + 1)
                cols = u.tiles * P
                at = u.tile * P
                fr = unit_ps[u.slot][1][:, 0:KT * cols].rearrange("p (k t) -> p k t", k=KT)
                nc.vector.tensor_tensor(h_lo[:, :, at:at + cols], fr, h_hi[:, :, at:at + cols].bitcast(F32),
                                        ALU.subtract).then_inc(h_lo_ready, 1)

            def shift(u):
                dve.wait_ge(logits_ready, u.n + 1)
                n = slice(0, u.tiles)
                lg = unit_ps[u.slot][0][:, 0:u.tiles * E].rearrange("p (n e) -> p n e", e=E)
                link(nc.vector.tensor_reduce(rowmax[u.slot][:, n], lg, AX.X, ALU.max))
                for t in range(u.tiles):
                    last = nc.vector.tensor_scalar(shifted[u.slot][:, t, :], lg[:, t, :], rowmax[u.slot][:, t:t + 1], None, ALU.subtract)
                last.then_inc(shifted_ready, 1)

            def choose(u):
                dve.wait_ge(expd_ready, u.n + 1)
                n = slice(0, u.tiles)
                for t in range(u.tiles):
                    last = nc.vector.max(top[u.slot][:, t, :], expd[u.slot][:, t, :])
                link(last)
                for t in range(u.tiles):
                    nc.vector.match_replace(out=replaced[u.slot][:, t, :], in_to_replace=top[u.slot][:, t, :],
                                            in_values=expd[u.slot][:, t, :], imm_value=-1.0)
                link(nc.vector.reduce_sum(top_sum[u.slot][:, 0, n], top[u.slot][:, n, :], AX.X))
                nc.vector.reciprocal(top_sum[u.slot][:, 1, n], top_sum[u.slot][:, 0, n])
                nc.vector.tensor_scalar(mask[u.slot][:, n, :], replaced[u.slot][:, n, :], 0.0, None, ALU.is_lt).then_inc(mask_ready, 1)
                dve.wait_ge(mask_ready, u.n + 1)
                for t in range(u.tiles):
                    last = nc.vector.scalar_tensor_tensor(out=wts[u.slot][:, t, :], in0=expd[u.slot][:, t, :],
                                                          scalar=top_sum[u.slot][:, 1, t:t + 1], in1=mask[u.slot][:, t, :],
                                                          op0=ALU.mult, op1=ALU.mult)
                link(last)

            def weigh(u):
                dve.wait_ge(ranks_ready, u.n + 1)
                s, n = u.slot, slice(0, u.tiles)
                if u.capped:
                    for t in range(u.tiles):
                        last = nc.vector.tensor_tensor(rank[s][:, t, :], unit_ps[s][1][:, t * E:(t + 1) * E], counts[:], ALU.add)
                    link(last)
                    link(nc.vector.scalar_tensor_tensor(out=wts[s][:, n, :], in0=rank[s][:, n, :], scalar=float(CAP),
                                                        in1=wts[s][:, n, :], op0=ALU.is_lt, op1=ALU.mult))
                link(nc.vector.tensor_tensor(counts[:], counts[:], unit_ps[s][1][:, NT * E:(NT + 1) * E], ALU.add))
                part = [parts[s][:, n, i * E:(i + 1) * E] for i in range(3)]
                link(nc.vector.tensor_copy(part[0], wts[s][:, n, :]))
                link(nc.vector.tensor_tensor(rest[s][:, n, :], wts[s][:, n, :], part[0], ALU.subtract))
                link(nc.vector.tensor_copy(part[1], rest[s][:, n, :]))
                nc.vector.tensor_tensor(part[2], rest[s][:, n, :], part[1], ALU.subtract).then_inc(parts_ready, 1)

            def spread_experts(u):
                if u.n:
                    return
                dve.wait_ge(consts_ready, 2)
                nc.vector.tensor_copy(spread[:], expert3[:, :, None].to_broadcast([3 * E, E, INTER])).then_inc(tables_ready, 1)

            for pair_at in range(0, len(units), 2):
                for stage in (stats_x, tables, norm_x, exponents, spread_experts, mix, add_mixed, norm_h, h_low, shift, choose, weigh):
                    for u in units[pair_at:pair_at + 2]:
                        stage(u)

            def step(n, k):
                dve.wait_ge(w_turned, n + 1)
                dve.wait_ge(s_ready, n + 1)
                dve.wait_ge(t_ready, n)
                nc.vector.tensor_tensor(t1_sb[:], w_ps[:], s_sb[:], ALU.mult).then_inc(t1_ready, 1)
                dve.wait_ge(t1_ready, n + 1)
                dve.wait_ge(u_ready, n + 1)
                dve.wait_ge(t_hi_ready, n)
                dve.wait_ge(t_lo_ready, n)
                nc.vector.tensor_tensor(t_sb[:], u_ps[:], t1_sb[:], ALU.mult).then_inc(t_ready, 1)
                dve.wait_ge(t_hi_ready, n + 1)
                dve.wait_ge(down_done, n)
                nc.vector.tensor_tensor(t_lo[k % 2][:], t_sb[:], t_hi[k % 2][:].bitcast(F32), ALU.subtract).then_inc(t_lo_ready, 1)

            for half in range(2):
                with dve.Fori(0, TURNS) as it:
                    for k in range(TURN_STEPS):
                        step(it * TURN_STEPS + (half * STEPS + k), k)
                dve.wait_ge(y_done, half + 1)
                if half:
                    dve.wait_ge(y_turned, half)
                nc.vector.tensor_copy(y_sb[:, 1, :], y_ps[1][:]).then_inc(y_copied, 1)
                dve.wait_ge(y_turned, half + 1)
                for t in range(HT):
                    at = half * HT + t
                    y = unit_ps[0][t // 2][:, (t % 2) * C:(t % 2 + 1) * C].rearrange("p (k c) -> p c k", k=KT)
                    rows = x1[:, at, :].rearrange("p (c k) -> p c k", k=KT)
                    last = nc.vector.tensor_tensor(rows, rows, y, ALU.add)
                last.then_inc(out_ready, 1)


_INS = ['x', 'ctx_2048', 'L0_xattn_w', 'L0_xattn_u', 'L0_ffn_gate_w', 'L0_ffn_w_gate', 'L0_ffn_w_up', 'L0_ffn_w_down']
_OUTS = [((16, 64, 256), 'float32')]


def kernel(**inputs):
    import numpy as _np
    import concourse.bacc as _bacc
    from concourse import mybir as _mybir
    from concourse.bass_utils import run_bass_kernel_spmd as _run

    nc = _bacc.Bacc("TRN2", target_bir_lowering=False, num_devices=1)
    arrays, args = {}, []
    for name in _INS:
        a = _np.ascontiguousarray(inputs[name])
        arrays[f"in_{name}_dram"] = a
        args.append(nc.dram_tensor(f"in_{name}_dram", a.shape, _mybir.dt.from_np(a.dtype), kind="ExternalInput").ap())
    for i, (shape, dtype) in enumerate(_OUTS):
        dt = _mybir.dt.from_np(_np.dtype(dtype))
        args.append(nc.dram_tensor(f"out_{i}_dram", shape, dt, kind="ExternalOutput").ap())
    program(nc, *args)
    r = _run(nc, [arrays], core_ids=[0])
    got = tuple(r.results[0][f"out_{i}_dram"] for i in range(len(_OUTS)))
    return got[0]
```

```python
from contextlib import ExitStack

import concourse.bass as bass
from concourse import mybir

F32 = mybir.dt.float32
F32R = mybir.dt.float32r
BF16 = mybir.dt.bfloat16
ALU = mybir.AluOpType
ACT = mybir.ActivationFunctionType
AX = mybir.AxisListType

P = 128
TOP = 8
EPS = 1e-5
START_MAX = -1e38
RESET = -2e38
NO_WEIGHT = -1e4


class Chain:

    def __init__(self, engine, sem):
        self.engine, self.sem, self.count, self.turn = engine, sem, 0, None

    def link(self, instruction):
        self.count += 1
        instruction.then_inc(self.sem, 1)
        at = self.count if self.turn is None else self.turn * self.per_turn + self.count
        self.engine.wait_ge(self.sem, at)

    def enter(self, turn, per_turn):
        self.turn, self.per_turn, self.entered = turn, per_turn, self.count

    def leave(self, turns):
        assert self.count - self.entered == self.per_turn, (self.count - self.entered, self.per_turn)
        self.count += (turns - 1) * self.per_turn
        self.turn = None


class Unit:

    def __init__(self, n, tile, tiles, slot, norms, capped):
        self.n, self.tile, self.tiles, self.slot = n, tile, tiles, slot
        self.first_norm, self.second_norm = norms
        self.capped = capped


def program(nc, x, ctx_in, decay, bonus, gate_w, w_gate, w_up, w_down, out):
    NB, S, C = x.shape
    E, _, INTER = w_gate.shape
    T = NB * S
    TILES = T // P
    HALF = T // 2
    HT = TILES // 2
    KT = C // P
    BPT = P // S
    NT = 2
    BK = NT * BPT * KT
    SP1 = S + 1
    CAP = 2 * (T * TOP // E)
    FT = E * INTER // P
    EG = 4
    GT = EG * INTER // P
    GF = EG * INTER
    GROUPS = E // EG
    assert GT * P == GF and CAP >= HALF and KT == 2 and GROUPS % 2 == 0
    PART = KT * GF
    assert PART == GT * C

    xt = x.rearrange("b s c -> (b s) c").rearrange("(n p) c -> p n c", p=P)
    ct = ctx_in.rearrange("b s c -> (b s) c").rearrange("(n p) c -> p n c", p=P)
    ot = out.rearrange("b s c -> (b s) c").rearrange("(n p) c -> p n c", p=P)
    wg_dram = w_gate.rearrange("e (p k) i -> p e (k i)", k=KT)
    wu_dram = w_up.rearrange("e (p k) i -> p e (k i)", k=KT)
    wd_dram = w_down.rearrange("e i c -> (e i) c").rearrange("(n p) c -> p n c", p=P)

    with ExitStack() as stack:
        def sb(name, shape, dt=F32):
            return stack.enter_context(nc.sbuf_tensor(name, shape, dt))

        def sem(name):
            return stack.enter_context(nc.semaphore(name))

        ident = sb("ident", [P, P])
        ident_bf = sb("ident_bf", [P, P], BF16)
        ones_bf = sb("ones_bf", [P, P], BF16)
        earlier = sb("earlier", [P, P], BF16)
        zeros_bf = sb("zeros_bf", [P, HALF], BF16)
        expert3 = sb("expert3", [3 * E, E], BF16)
        spread = sb("spread", [3 * E, E, INTER], BF16)
        neg_half = sb("neg_half", [P, HT])
        decay_sb = sb("decay_sb", [P, KT])
        bonus_sb = sb("bonus_sb", [P, KT])
        decays = sb("decays", [P, BK, SP1])
        gate_sb = sb("gate_sb", [P, KT, E])
        gate_hi = sb("gate_hi", [P, KT, E], F32R)
        gate_lo = sb("gate_lo", [P, KT, E], F32R)
        x_sb = sb("x_sb", [P, TILES, C])
        ctx_sb = sb("ctx_sb", [P, HT, C])
        ctx_tile = sb("ctx_tile", [P, 1, C])
        x1 = sb("x1", [P, TILES, C])
        h_hi = sb("h_hi", [P, KT, T], F32R)
        h_lo = sb("h_lo", [P, KT, T], F32R)
        route = sb("route", [3 * E, T], BF16)
        counts = sb("counts", [P, E])
        def sets(name, shape, dt=F32):
            return [sb(f"{name}{i}", shape(n), dt) for i, n in enumerate((NT, NT, 1))]

        PAIRS = BPT * KT
        stats, mv = sets("stats", lambda n: [P, n, 6]), sets("mv", lambda n: [P, n, 2])
        var, rstd = sets("var", lambda n: [P, n]), sets("rstd", lambda n: [P, n])
        normed = sets("normed", lambda n: [P, n, C])
        kpad, vpad, opad, ev2 = (sets(name, lambda n: [P, n * PAIRS, SP1]) for name in ("kpad", "vpad", "opad", "ev2"))
        diffs = sets("diffs", lambda n: [P, 2, n * PAIRS, S])
        expo = sets("expo", lambda n: [P, 4, n * PAIRS, SP1])
        fact = expo[0:2] + [sb("fact2", [P, 4, PAIRS, SP1])]
        state = sets("state", lambda n: [P, 2, n * PAIRS, SP1])
        mixed = sets("mixed", lambda n: [P, KT * n * P])
        shifted, expd, replaced, rank, wts, rest = (
            sets(name, lambda n: [P, n, E]) for name in ("shifted", "expd", "replaced", "rank", "wts", "rest"))
        top, top_sum, rowmax = sets("top", lambda n: [P, n, TOP]), sets("top_sum", lambda n: [P, 2, n]), sets("rowmax", lambda n: [P, n])
        mask = sets("mask", lambda n: [P, n, E], BF16)
        parts = sets("parts", lambda n: [P, n, 3 * E], BF16)
        tile_hi = sb("tile_hi", [P, KT, P], F32R)
        tile_lo = sb("tile_lo", [P, KT, P], F32R)
        raw = [sb(f"raw{i}", [P, 3, PART]) for i in range(2)]
        whi = [sb(f"whi{i}", [P, 3, PART], F32R) for i in range(2)]
        wlo = [sb(f"wlo{i}", [P, 3, PART], F32R) for i in range(2)]
        s_sb = sb("s_sb", [P, HALF])
        t1_sb = sb("t1_sb", [P, HALF])
        t_sb = sb("t_sb", [P, HALF])
        t_hi = [sb(f"t_hi{i}", [P, HALF], F32R) for i in range(2)]
        t_lo = [sb(f"t_lo{i}", [P, HALF], F32R) for i in range(2)]
        y_sb = sb("y_sb", [P, KT, HALF])

        bank = [stack.enter_context(nc.psum_tensor(f"bank{i}", [P, 512], F32)) for i in range(8)]
        y_ps, g_ps, u_ps, w_ps = bank[0:2], bank[2], bank[3], bank[4]

        class Places:

            def __init__(self, k, v, h, logits, ranks, parts):
                self.k, self.v, self.mixed, self.h, self.logits, self.ranks = k, v, k, h, logits, ranks
                self.parts = parts.bitcast(BF16)

        ps = [Places(bank[i], bank[i + 1], bank[i + 1], bank[i], bank[i + 1], bank[i]) for i in (0, 2)]
        ps.append(Places(bank[5], bank[6], bank[7][:, 0:KT * P], bank[7][:, 256:256 + E],
                         bank[7][:, 288:288 + 2 * E], bank[7][:, 384:384 + P // 2]))
        out_ps = bank[5:7]

        x_landed = [sem(f"x_landed{i}") for i in range(3)]
        ctx_landed, tile_landed = sem("ctx_landed"), sem("tile_landed")
        small_landed = sem("small_landed")
        raw_landed = [sem(f"raw_landed{i}") for i in range(2)]
        out_stored = sem("out_stored")
        pool_chain, dve_chain, act_chain = sem("pool_chain"), sem("dve_chain"), sem("act_chain")
        consts_ready, settled, tables_ready = sem("consts_ready"), sem("settled"), sem("tables_ready")
        gate_hi_ready, gate_ready = sem("gate_hi_ready"), sem("gate_ready")
        var_ready, rstd_ready = sem("var_ready"), sem("rstd_ready")
        k_normed, kv_turned, kv_ready = sem("k_normed"), sem("kv_turned"), sem("kv_ready")
        expo_ready, fact_ready, mixed_ready, mixed_turned = sem("expo_ready"), sem("fact_ready"), sem("mixed_ready"), sem("mixed_turned")
        h_normed, h_turned, h_hi_ready, h_lo_ready = sem("h_normed"), sem("h_turned"), sem("h_hi_ready"), sem("h_lo_ready")
        logits_ready, shifted_ready, expd_ready = sem("logits_ready"), sem("shifted_ready"), sem("expd_ready")
        mask_ready, ranks_ready, parts_ready, parts_turned, route_ready = sem("mask_ready"), sem("ranks_ready"), sem("parts_ready"), sem("parts_turned"), sem("route_ready")
        ev_ready, h_lo_kept = sem("ev_ready"), sem("h_lo_kept")
        w_hi_ready, w_lo_ready = sem("w_hi_ready"), sem("w_lo_ready")
        w_turned, g_ready, u_ready, down_done = sem("w_turned"), sem("g_ready"), sem("u_ready"), sem("down_done")
        s_ready, t1_ready, t_ready, t_hi_ready, t_lo_ready = sem("s_ready"), sem("t1_ready"), sem("t_ready"), sem("t_hi_ready"), sem("t_lo_ready")
        y_done, y_copied, y_turned, out_ready = sem("y_done"), sem("y_copied"), sem("y_turned"), sem("out_ready")

        first_units = [Unit(n, NT * n, NT, n, (n, n + 3), False) for n in range(2)]
        LATER = HT

        def later(n):
            return Unit(n, n + 2, 1, 2, (n * 2, n * 2 + 1), True)

        early = Unit(2, HT, 1, 2, (2, 5), True)
        UNITS = 2 + LATER
        TURNS = GROUPS // 2
        STEPS = GROUPS * GT
        TURN_STEPS = 2 * GT

        def raw_parts(slot, part):
            r = raw[slot][:, part, :]
            if part < 2:
                return r.rearrange("p (e k i) -> p k e i", e=EG, k=KT)
            return r

        def split_view(w, slot, part):
            v = w[slot][:, part, :]
            if part < 2:
                return v.rearrange("p (k e i) -> p k e i", e=EG, k=KT)
            return v

        def up_weight(w, slot, part, k, j):
            at = k * GF + j * P
            return w[slot][:, part, at:at + P]

        def down_weight(w, slot, j, m):
            return w[slot][:, 2, j * C:(j + 1) * C].rearrange("p (c k) -> p k c", k=KT)[:, m, :]

        block = stack.enter_context(nc.Block())

        @block.sync
        def _(sp):
            for u in first_units:
                sp.dma_start(x_sb[:, u.tile:u.tile + NT, :], xt[:, u.tile:u.tile + NT, :]).then_inc(x_landed[u.n], 16)
            sp.dma_start(x_sb[:, HT:, :], xt[:, HT:, :]).then_inc(x_landed[2], 16)

            def load(slot, group):
                experts = bass.ds(group * EG, EG)
                for part, w in ((0, wg_dram), (1, wu_dram)):
                    sp.dma_start(raw[slot][:, part, :].rearrange("p (e n) -> p e n", e=EG),
                                 w[:, experts, :]).then_inc(raw_landed[slot], 16)
                sp.dma_start(raw[slot][:, 2, :].rearrange("p (n c) -> p n c", n=GT),
                             wd_dram[:, bass.ds(group * GT, GT), :]).then_inc(raw_landed[slot], 16)

            sp.dma_start(ctx_tile[:], ct[:, HT:HT + 1, :]).then_inc(tile_landed, 16)
            load(0, 0)
            load(1, 1)
            def load_context(n):
                sp.wait_ge(kv_turned, n)
                sp.dma_start(ctx_tile[:], ct[:, bass.ds(n + 2, 1), :]).then_inc(tile_landed, 16)

            def reload(half, slot, it, group):
                done = it * 6 + (half * GROUPS + slot + 1) * 3
                sp.wait_ge(w_hi_ready, done)
                sp.wait_ge(w_lo_ready, done)
                load(slot, group)

            for half in range(2):
                with sp.Fori(0, TURNS - 1) as it:
                    if half == 0:
                        load_context(it + 3)
                    for slot in range(2):
                        reload(half, slot, it, it * 2 + (2 + slot))
                if half == 0:
                    for slot in range(2):
                        reload(half, slot, TURNS - 1, slot)
            for half in range(2):
                sp.wait_ge(out_ready, half + 1)
                tiles = slice(half * HT, (half + 1) * HT)
                sp.dma_start(ot[:, tiles, :], x1[:, tiles, :]).then_inc(out_stored, 16)
            sp.wait_ge(out_stored, 32)

        @block.gpsimd
        def _(pool):
            chain = Chain(pool, pool_chain)
            pool.memset(ident[:], 0.0)
            pool.memset(ident_bf[:], 0.0)
            pool.memset(expert3[:], 0.0)
            pool.memset(zeros_bf[:], 0.0)
            pool.memset(ones_bf[:], 1.0)
            chain.link(pool.memset(earlier[:], 1.0))
            pool.affine_select(out=ident[:], in_=ident[:], compare_op=ALU.not_equal, fill=1.0, base=0,
                               pattern=[[-1, P]], channel_multiplier=1).then_inc(consts_ready, 1)
            pool.affine_select(out=ident_bf[:], in_=ident_bf[:], compare_op=ALU.not_equal, fill=1.0, base=0,
                               pattern=[[-1, P]], channel_multiplier=1)
            pool.affine_select(out=earlier[:], in_=earlier[:], compare_op=ALU.is_gt, fill=0.0, base=0,
                               pattern=[[1, P]], channel_multiplier=-1)
            for part in range(3):
                chain.link(pool.affine_select(out=expert3[:], in_=expert3[:], compare_op=ALU.not_equal, fill=1.0,
                                              base=-part * E, pattern=[[-1, E]], channel_multiplier=1))
            pool.memset(neg_half[:], -0.5).then_inc(consts_ready, 1)

            def split_low(slot, part, group):
                pool.wait_ge(w_hi_ready, group * 3 + part + 1)
                if not isinstance(group, int) or group >= 2:
                    pool.wait_ge(down_done, (group - 1) * GT + 1)
                pool.tensor_tensor(split_view(wlo, slot, part), raw_parts(slot, part),
                                   split_view(whi, slot, part).bitcast(F32), ALU.subtract).then_inc(w_lo_ready, 1)

            pool.wait_ge(consts_ready, 2)
            def power(u, norm):
                pool.wait_ge(var_ready, norm + 1)
                pool.tensor_tensor(rstd[u.slot][:], var[u.slot][:], neg_half[:, 0:u.tiles], ALU.pow).then_inc(rstd_ready, 1)

            def new_values(u):
                pool.wait_ge(fact_ready, u.n + 1)
                pool.tensor_tensor(opad[u.slot][:, :, 1:], fact[u.slot][:, 0, :, 1:], vpad[u.slot][:, :, 1:],
                                   ALU.mult).then_inc(ev_ready, 1)

            def keep_low(u):
                pool.wait_ge(h_lo_ready, u.n + 1)
                pool.tensor_copy(h_lo[:, :, bass.ds(u.tile * P, P)], tile_lo[:].bitcast(F32)).then_inc(h_lo_kept, 1)

            for u in (*first_units, early):
                power(u, u.first_norm)
            for u in (*first_units, early):
                new_values(u)
            for u in (*first_units, early):
                power(u, u.second_norm)
            for part in range(3):
                split_low(0, part, 0)

            def turn(half, it, front, back, final=False):
                for k in range(TURN_STEPS):
                    if front and k == 0:
                        power(front, front.first_norm)
                    ahead = k // GT + 1
                    if ahead == 1 or not final:
                        split_low(ahead % 2, k % GT, it * 2 + (half * GROUPS + ahead))
                    if back and k == 0:
                        keep_low(back)
                    if front and k == 2:
                        new_values(front)
                    if front and k == 4:
                        power(front, front.second_norm)

            with pool.Fori(0, TURNS - 1) as it:
                turn(0, it, later(it + 3), later(it + 2))
            turn(0, TURNS - 1, None, later(TURNS + 1))
            with pool.Fori(0, TURNS - 1) as it:
                turn(1, it, None, None)
            turn(1, TURNS - 1, None, None, final=True)

        @block.scalar
        def _(act):
            act.dma_start(ctx_sb[:], ct[:, 0:HT, :]).then_inc(ctx_landed, 16)
            act.dma_start(decay_sb[:], decay.rearrange("(p k) -> p k", k=KT)).then_inc(small_landed, 16)
            act.dma_start(bonus_sb[:], bonus.rearrange("(p k) -> p k", k=KT)).then_inc(small_landed, 16)
            act.dma_start(gate_sb[:], gate_w.rearrange("(p k) e -> p k e", k=KT)).then_inc(small_landed, 16)
            act.wait_ge(small_landed, 48)
            nc.scalar.activation(gate_hi[:], gate_sb[:], ACT.Copy).then_inc(gate_hi_ready, 1)

            def take_kv(u):
                act.wait_ge(kv_turned, u.n + 1)
                for at, pad in ((ps[u.slot].k, kpad), (ps[u.slot].v, vpad)):
                    to = pad[u.slot][:, :, 1:].rearrange("p (b k) s -> p k b s", k=KT)
                    fr = at[:, 0:KT * u.tiles * P].rearrange("p (k b s) -> p k b s", k=KT, s=S)
                    last = nc.scalar.activation(to, fr, ACT.Copy)
                last.then_inc(kv_ready, 1)

            def exps(u):
                act.wait_ge(expo_ready, u.n + 1)
                nc.scalar.activation(fact[u.slot][:], expo[u.slot][:], ACT.Exp).then_inc(fact_ready, 1)

            def take_h(u):
                act.wait_ge(h_turned, u.n + 1)
                cols = u.tiles * P
                fr = ps[u.slot].h[:, 0:KT * cols].rearrange("p (k t) -> p k t", k=KT)
                if u.slot < 2:
                    at = u.tile * P
                    nc.scalar.activation(h_hi[:, :, at:at + cols], fr, ACT.Copy).then_inc(h_hi_ready, 1)
                else:
                    nc.scalar.activation(tile_hi[:], fr, ACT.Copy).then_inc(h_hi_ready, 1)
                    act.wait_ge(h_hi_ready, u.n + 1)
                    nc.scalar.activation(h_hi[:, :, bass.ds(u.tile * P, P)], tile_hi[:].bitcast(F32), ACT.Copy)

            def route_exps(u):
                act.wait_ge(shifted_ready, u.n + 1)
                nc.scalar.activation(expd[u.slot][:], shifted[u.slot][:], ACT.Exp).then_inc(expd_ready, 1)

            def take_route(u):
                act.wait_ge(parts_turned, u.n + 1)
                cols = u.tiles * P
                fr = ps[u.slot].parts[0:3 * E, 0:cols]
                nc.scalar.activation(route[:, bass.ds(u.tile * P, cols)], fr, ACT.Copy).then_inc(route_ready, 1)

            def split_high(slot, part, group):
                act.wait_ge(raw_landed[slot], group * 24 + (48 - slot * 24))
                if not isinstance(group, int) or group >= 2:
                    act.wait_ge(down_done, (group - 1) * GT + 1)
                nc.scalar.activation(split_view(whi, slot, part), raw_parts(slot, part), ACT.Copy).then_inc(w_hi_ready, 1)

            for stage in (take_kv, exps, take_h, route_exps, take_route):
                for u in (*first_units, early) if stage in (take_kv, exps) else first_units:
                    stage(u)
                if stage is take_kv:
                    for part in range(3):
                        split_high(0, part, 0)

            def step(n, k):
                act.wait_ge(g_ready, n + 1)
                act.wait_ge(t1_ready, n)
                nc.scalar.activation(s_sb[:], g_ps[:], ACT.Silu).then_inc(s_ready, 1)
                act.wait_ge(t_ready, n + 1)
                act.wait_ge(down_done, n)
                nc.scalar.activation(t_hi[k % 2][:], t_sb[:], ACT.Copy).then_inc(t_hi_ready, 1)

            def turn(half, it, front, back, final=False):
                for k in range(TURN_STEPS):
                    step(it * TURN_STEPS + (half * STEPS + k), k)
                    if back and k == 0:
                        take_h(back)
                    if front and k == 1:
                        take_kv(front)
                    if back and k == 2:
                        route_exps(back)
                    if front and k == 2:
                        exps(front)
                    ahead = k // GT + 1
                    if ahead == 1 or not final:
                        split_high(ahead % 2, k % GT, it * 2 + (half * GROUPS + ahead))
                    if back and k == TURN_STEPS - 1:
                        take_route(back)

            for half in range(2):
                with act.Fori(0, TURNS - 1) as it:
                    turn(half, it, None if half else later(it + 3), None if half else later(it + 2))
                turn(half, TURNS - 1, None, None if half else later(TURNS + 1), final=half == 1)
                act.wait_ge(y_done, half + 1)
                if half:
                    act.wait_ge(y_turned, half)
                nc.scalar.activation(y_sb[:, 0, :], y_ps[0][:], ACT.Copy).then_inc(y_copied, 1)

        @block.tensor
        def _(pe):
            def turn_kv(u):
                if u is first_units[0]:
                    pe.wait_ge(consts_ready, 1)
                pe.wait_ge(k_normed, u.n + 1)
                if u.slot < 2:
                    pe.wait_ge(ctx_landed, 16)
                    context = ctx_sb[:, u.tile:u.tile + u.tiles, :]
                else:
                    pe.wait_ge(tile_landed, (u.n - 1) * 16)
                    if u is not early:
                        pe.wait_ge(h_normed, u.n)
                    context = ctx_tile[:]
                for to, src in ((ps[u.slot].k, normed[u.slot][:]), (ps[u.slot].v, context)):
                    for t in range(u.tiles):
                        rows = src[:, t, :].rearrange("p (c k) -> p k c", k=KT)
                        for k in range(KT):
                            at = (k * u.tiles + t) * P
                            last = nc.tensor.transpose(to[:, at:at + P], rows[:, k, :], ident[:])
                last.then_inc(kv_turned, 1)

            def turn_mixed(u):
                pe.wait_ge(mixed_ready, u.n + 1)
                for t in range(u.tiles):
                    for k in range(KT):
                        at = (t * KT + k) * P
                        last = nc.tensor.transpose(ps[u.slot].mixed[:, at:at + P],
                                                   mixed[u.slot][:, (k * u.tiles + t) * P:(k * u.tiles + t + 1) * P], ident[:])
                last.then_inc(mixed_turned, 1)

            def turn_h(u):
                pe.wait_ge(h_normed, u.n + 1)
                if u.slot == 2 and u is not early:
                    pe.wait_ge(route_ready, u.n)
                for t in range(u.tiles):
                    rows = normed[u.slot][:, t, :].rearrange("p (c k) -> p k c", k=KT)
                    for k in range(KT):
                        at = (k * u.tiles + t) * P
                        last = nc.tensor.transpose(ps[u.slot].h[:, at:at + P], rows[:, k, :], ident[:])
                last.then_inc(h_turned, 1)

            def logits(u):
                pe.wait_ge(h_hi_ready, u.n + 1)
                pe.wait_ge(h_lo_ready, u.n + 1)
                if u is first_units[0]:
                    pe.wait_ge(gate_ready, 1)
                for t in range(u.tiles):
                    if u.slot < 2:
                        cols = slice((u.tile + t) * P, (u.tile + t + 1) * P)
                        hi, lo = h_hi[:, :, cols], h_lo[:, :, cols]
                    else:
                        hi, lo = tile_hi[:], tile_lo[:]
                    terms = [(a, b, k) for k in range(KT) for a, b in ((hi, gate_hi), (hi, gate_lo), (lo, gate_hi))]
                    for n, (a, b, k) in enumerate(terms):
                        last = nc.tensor.matmul(ps[u.slot].logits[:, t * E:(t + 1) * E], a[:, k, :], b[:, k, :],
                                                start=(n == 0), stop=(n == len(terms) - 1))
                last.then_inc(logits_ready, 1)

            def ranks(u):
                pe.wait_ge(mask_ready, u.n + 1)
                if u is first_units[0]:
                    pe.wait_ge(consts_ready, 2)
                to = ps[u.slot].ranks
                if u.capped:
                    for t in range(u.tiles):
                        for s in range(t + 1):
                            nc.tensor.matmul(to[:, t * E:(t + 1) * E], (earlier if s == t else ones_bf)[:], mask[u.slot][:, s, :],
                                             start=(s == 0), stop=(s == t))
                for s in range(u.tiles):
                    last = nc.tensor.matmul(to[:, u.tiles * E:(u.tiles + 1) * E], ones_bf[:], mask[u.slot][:, s, :],
                                            start=(s == 0), stop=(s == u.tiles - 1))
                last.then_inc(ranks_ready, 1)

            def turn_parts(u):
                pe.wait_ge(parts_ready, u.n + 1)
                to = ps[u.slot].parts
                for t in range(u.tiles):
                    last = nc.tensor.transpose(to[0:3 * E, t * P:(t + 1) * P], parts[u.slot][:, t, :], ident_bf[:])
                last.then_inc(parts_turned, 1)

            for stage in (turn_kv, turn_mixed, turn_h, logits, ranks, turn_parts):
                for u in (*first_units, early) if stage in (turn_kv, turn_mixed) else first_units:
                    stage(u)

            def up(n, half, slot, j, tile, group):
                tokens = slice(half * HALF, (half + 1) * HALF)
                pe.wait_ge(t1_ready, n)
                nc.tensor.matmul(w_ps[:], spread[:].rearrange("p e i -> p (e i)")[:, bass.ds(tile * P, P)],
                                 route[:, tokens], start=True, stop=True).then_inc(w_turned, 1)
                pe.wait_ge(s_ready, n)
                for part, ps, ready in ((0, g_ps, g_ready), (1, u_ps, u_ready)):
                    if part == 1:
                        pe.wait_ge(t_ready, n)
                    if j == 0:
                        pe.wait_ge(w_hi_ready, group * 3 + (part + 1))
                        pe.wait_ge(w_lo_ready, group * 3 + (part + 1))
                    terms = [(w, h, k) for k in range(KT) for w, h in ((whi, h_hi), (whi, h_lo), (wlo, h_hi))]
                    for i, (w, h, k) in enumerate(terms):
                        last = nc.tensor.matmul(ps[:], up_weight(w, slot, part, k, j), h[:, k, tokens],
                                                start=(i == 0), stop=(i == len(terms) - 1))
                    last.then_inc(ready, 1)

            def down(n, slot, j, odd, group):
                if j == 0:
                    pe.wait_ge(w_hi_ready, group * 3 + 3)
                    pe.wait_ge(w_lo_ready, group * 3 + 3)
                pe.wait_ge(t_hi_ready, n + 1)
                for m in range(KT):
                    nc.tensor.matmul(y_ps[m][:], down_weight(whi, slot, j, m), t_hi[odd][:], start=False, stop=False)
                    nc.tensor.matmul(y_ps[m][:], down_weight(wlo, slot, j, m), t_hi[odd][:], start=False, stop=False)
                pe.wait_ge(t_lo_ready, n + 1)
                for m in range(KT):
                    last = nc.tensor.matmul(y_ps[m][:], down_weight(whi, slot, j, m), t_lo[odd][:], start=False, stop=False)
                last.then_inc(down_done, 1)

            for half in range(2):
                pe.wait_ge(route_ready, UNITS if half else len(first_units))
                if half == 0:
                    pe.wait_ge(tables_ready, 1)
                else:
                    pe.wait_ge(h_lo_kept, LATER)
                    pe.wait_ge(y_copied, 2 * half)
                for m in range(KT):
                    first = nc.tensor.matmul(y_ps[m][:], zeros_bf[:, 0:P], zeros_bf[:], start=True, stop=False)
                if half == 0:
                    first.then_inc(down_done, 1)

                def turn(it, first_turn, front, back):
                    for k in range(TURN_STEPS):
                        n = it * TURN_STEPS + (half * STEPS + k)
                        slot, j = k // GT, k % GT
                        up(n, half, slot, j, it * TURN_STEPS + k, it * 2 + (half * GROUPS + slot))
                        if back and k == 0:
                            turn_h(back)
                        if front and k == 1:
                            turn_kv(front)
                        if back and k == 1:
                            logits(back)
                        if back and k == 3:
                            ranks(back)
                        if back and k == 5:
                            turn_parts(back)
                        if k > 0:
                            down(n - 1, (k - 1) // GT, (k - 1) % GT, (k - 1) % 2, it * 2 + (half * GROUPS + (k - 1) // GT))
                        elif not first_turn:
                            down(n - 1, 1, GT - 1, 1, None)
                        if front and k == 4:
                            turn_mixed(front)

                if half == 0:
                    turn(0, True, later(3), later(2))
                    with pe.Fori(1, TURNS - 1) as it:
                        turn(it, False, later(it + 3), later(it + 2))
                    turn(TURNS - 1, False, None, later(TURNS + 1))
                else:
                    turn(0, True, None, None)
                    with pe.Fori(1, TURNS) as it:
                        turn(it, False, None, None)
                down(half * STEPS + STEPS - 1, 1, GT - 1, 1, None)
                for m in range(KT):
                    last = nc.tensor.matmul(y_ps[m][:], zeros_bf[:, 0:P], zeros_bf[:], start=False, stop=True)
                last.then_inc(y_done, 1)
                pe.wait_ge(y_copied, 2 * (half + 1))
                if half:
                    pe.wait_ge(out_ready, half)
                for t in range(HT):
                    to = out_ps[t // 2]
                    for k in range(KT):
                        at = ((t % 2) * KT + k) * P
                        last = nc.tensor.transpose(to[:, at:at + P], y_sb[:, k, t * P:(t + 1) * P], ident[:])
                last.then_inc(y_turned, 1)

        @block.vector
        def _(dve):
            chain = Chain(dve, dve_chain)
            link = chain.link
            for s in range(3):
                nc.vector.memset(kpad[s][:, :, 0:1], START_MAX)
                nc.vector.memset(vpad[s][:, :, 0:1], 0.0)
                for q in range(4):
                    nc.vector.memset(expo[s][:, q, :, 0:1], NO_WEIGHT)
            nc.vector.memset(counts[:], 0.0)
            link(nc.vector.memset(decays[:], 0.0))

            def settle():
                dve.sem_inc(settled, 1)

            def link_settled(instruction):
                chain.link(instruction)
                settle()

            def norm_stats(u, src):
                for t in range(u.tiles):
                    last = nc.vector.bn_stats(stats[u.slot][:, t, :], src[:, u.tile + t, :])
                link_settled(last)
                for t in range(u.tiles):
                    last = nc.vector.bn_aggr(mv[u.slot][:, t, :], stats[u.slot][:, t, :])
                link(last)
                nc.vector.tensor_scalar(var[u.slot][:], mv[u.slot][:, :, 1], EPS, None, ALU.add).then_inc(var_ready, 1)

            def norm_apply(u, src, ready, norm):
                dve.wait_ge(rstd_ready, norm + 1)
                for t in range(u.tiles):
                    last = nc.vector.tensor_scalar(normed[u.slot][:, t, :], src[:, u.tile + t, :], mv[u.slot][:, t, 0:1],
                                                   rstd[u.slot][:, t:t + 1], ALU.subtract, ALU.mult)
                last.then_inc(ready, 1)

            def stats_x(u):
                dve.wait_ge(x_landed[u.slot], 16)
                norm_stats(u, x_sb)

            def norm_x(u):
                norm_apply(u, x_sb, k_normed, u.first_norm)

            def tables(u):
                if u is not first_units[0]:
                    return
                dve.wait_ge(small_landed, 48)
                dve.wait_ge(gate_hi_ready, 1)
                nc.vector.tensor_tensor(gate_lo[:], gate_sb[:], gate_hi[:].bitcast(F32), ALU.subtract).then_inc(gate_ready, 1)
                by = decays[:].rearrange("p (b k) s -> p b k s", k=KT)
                for k in range(KT):
                    nc.vector.tensor_scalar(by[:, :, k, 1:], by[:, :, k, 1:], decay_sb[:, k:k + 1], None, ALU.add)
                link(nc.vector.memset(decays[:, :, 0:1], RESET))

            def exponents(u):
                dve.wait_ge(kv_ready, u.n + 1)
                bk = u.tiles * BPT * KT
                k_, o_ = kpad[u.slot][:], opad[u.slot][:]
                flat = lambda a: a.rearrange("p b s -> p (b s)")
                link(nc.vector.tensor_tensor_scan(flat(o_), flat(decays[:, 0:bk, :]), flat(k_), 0.0, ALU.add, ALU.max))
                for k in range(KT):
                    now = k_.rearrange("p (b k) s -> p b k s", k=KT)[:, :, k, 1:]
                    was = o_.rearrange("p (b k) s -> p b k s", k=KT)[:, :, k, 0:S]
                    d = diffs[u.slot][:].rearrange("p q (b k) s -> p q b k s", k=KT)
                    nc.vector.scalar_tensor_tensor(out=d[:, 0, :, k, :], in0=now, scalar=bonus_sb[:, k:k + 1], in1=was,
                                                   op0=ALU.add, op1=ALU.subtract)
                    last = nc.vector.scalar_tensor_tensor(out=d[:, 1, :, k, :], in0=was, scalar=decay_sb[:, k:k + 1], in1=now,
                                                          op0=ALU.add, op1=ALU.subtract)
                link(last)
                nc.vector.tensor_scalar(expo[u.slot][:, 0:2, :, 1:], diffs[u.slot][:], 0.0, None, ALU.min)
                nc.vector.tensor_scalar(expo[u.slot][:, 2:4, :, 1:], diffs[u.slot][:], -1.0, 0.0,
                                        ALU.mult, ALU.min).then_inc(expo_ready, 1)

            def states(u):
                dve.wait_ge(fact_ready, u.n + 1)
                st = state[u.slot]
                flat = lambda v: v.rearrange("p b s -> p (b s)")
                e, a2, a, e2 = (fact[u.slot][:, q] for q in range(4))
                link(nc.vector.tensor_tensor(ev2[u.slot][:], e2, vpad[u.slot][:], ALU.mult))
                nc.vector.tensor_tensor_scan(flat(st[:, 0]), flat(a2), flat(ev2[u.slot][:]), 0.0, ALU.mult, ALU.add)
                link(nc.vector.tensor_tensor_scan(flat(st[:, 1]), flat(a2), flat(e2), 0.0, ALU.mult, ALU.add))
                for q in range(2):
                    last = nc.vector.tensor_tensor(diffs[u.slot][:, q], a[:, :, 1:], st[:, q, :, 0:S], ALU.mult)
                link(last)

            def mix(u):
                dve.wait_ge(ev_ready, u.n + 1)
                num, den = (diffs[u.slot][:, q] for q in range(2))
                nc.vector.tensor_tensor(num, num, opad[u.slot][:, :, 1:], ALU.add)
                link(nc.vector.tensor_tensor(den, den, fact[u.slot][:, 0, :, 1:], ALU.add))
                link(nc.vector.reciprocal(den, den))
                by_token = lambda v: v.rearrange("p (b k) s -> p b k s", k=KT)
                y = mixed[u.slot][:].rearrange("p (k b s) -> p b k s", k=KT, s=S)
                nc.vector.tensor_tensor(y, by_token(num), by_token(den), ALU.mult).then_inc(mixed_ready, 1)

            def add_mixed(u):
                dve.wait_ge(mixed_turned, u.n + 1)
                for t in range(u.tiles):
                    y = ps[u.slot].mixed[:, t * C:(t + 1) * C].rearrange("p (k c) -> p c k", k=KT)
                    last = nc.vector.tensor_tensor(x1[:, u.tile + t, :].rearrange("p (c k) -> p c k", k=KT),
                                                   x_sb[:, u.tile + t, :].rearrange("p (c k) -> p c k", k=KT), y, ALU.add)
                link_settled(last)
                norm_stats(u, x1)

            def norm_h(u):
                norm_apply(u, x1, h_normed, u.second_norm)

            def h_low(u):
                dve.wait_ge(h_hi_ready, u.n + 1)
                cols = slice(u.tile * P, (u.tile + u.tiles) * P) if u.slot < 2 else None
                fr = ps[u.slot].h[:, 0:KT * u.tiles * P].rearrange("p (k t) -> p k t", k=KT)
                hi, lo = (h_hi[:, :, cols], h_lo[:, :, cols]) if u.slot < 2 else (tile_hi[:], tile_lo[:])
                nc.vector.tensor_tensor(lo, fr, hi.bitcast(F32), ALU.subtract).then_inc(h_lo_ready, 1)

            def shift(u):
                dve.wait_ge(logits_ready, u.n + 1)
                n = slice(0, u.tiles)
                lg = ps[u.slot].logits[:, 0:u.tiles * E].rearrange("p (n e) -> p n e", e=E)
                link(nc.vector.tensor_reduce(rowmax[u.slot][:, n], lg, AX.X, ALU.max))
                for t in range(u.tiles):
                    last = nc.vector.tensor_scalar(shifted[u.slot][:, t, :], lg[:, t, :], rowmax[u.slot][:, t:t + 1], None, ALU.subtract)
                last.then_inc(shifted_ready, 1)

            def choose(u):
                dve.wait_ge(expd_ready, u.n + 1)
                settle()
                n = slice(0, u.tiles)
                for t in range(u.tiles):
                    last = nc.vector.max(top[u.slot][:, t, :], expd[u.slot][:, t, :])
                link_settled(last)
                for t in range(u.tiles):
                    nc.vector.match_replace(out=replaced[u.slot][:, t, :], in_to_replace=top[u.slot][:, t, :],
                                            in_values=expd[u.slot][:, t, :], imm_value=-1.0)
                link(nc.vector.reduce_sum(top_sum[u.slot][:, 0, n], top[u.slot][:, n, :], AX.X))
                nc.vector.reciprocal(top_sum[u.slot][:, 1, n], top_sum[u.slot][:, 0, n])
                nc.vector.tensor_scalar(mask[u.slot][:, n, :], replaced[u.slot][:, n, :], 0.0, None, ALU.is_lt).then_inc(mask_ready, 1)
                dve.wait_ge(mask_ready, u.n + 1)
                for t in range(u.tiles):
                    last = nc.vector.scalar_tensor_tensor(out=wts[u.slot][:, t, :], in0=expd[u.slot][:, t, :],
                                                          scalar=top_sum[u.slot][:, 1, t:t + 1], in1=mask[u.slot][:, t, :],
                                                          op0=ALU.mult, op1=ALU.mult)
                link(last)

            def weigh(u):
                dve.wait_ge(ranks_ready, u.n + 1)
                s, n = u.slot, slice(0, u.tiles)
                if u.capped:
                    for t in range(u.tiles):
                        last = nc.vector.tensor_tensor(rank[s][:, t, :], ps[s].ranks[:, t * E:(t + 1) * E], counts[:], ALU.add)
                    link(last)
                    link(nc.vector.scalar_tensor_tensor(out=wts[s][:, n, :], in0=rank[s][:, n, :], scalar=float(CAP),
                                                        in1=wts[s][:, n, :], op0=ALU.is_lt, op1=ALU.mult))
                link(nc.vector.tensor_tensor(counts[:], counts[:], ps[s].ranks[:, u.tiles * E:(u.tiles + 1) * E], ALU.add))
                part = [parts[s][:, n, i * E:(i + 1) * E] for i in range(3)]
                link(nc.vector.tensor_copy(part[0], wts[s][:, n, :]))
                link(nc.vector.tensor_tensor(rest[s][:, n, :], wts[s][:, n, :], part[0], ALU.subtract))
                link(nc.vector.tensor_copy(part[1], rest[s][:, n, :]))
                nc.vector.tensor_tensor(part[2], rest[s][:, n, :], part[1], ALU.subtract).then_inc(parts_ready, 1)

            def spread_experts(u):
                if u is not first_units[0]:
                    return
                dve.wait_ge(consts_ready, 2)
                nc.vector.tensor_copy(spread[:], expert3[:, :, None].to_broadcast([3 * E, E, INTER])).then_inc(tables_ready, 1)

            for stage in (stats_x, tables, norm_x, exponents, spread_experts, states, mix, add_mixed, norm_h):
                for u in (*first_units, early):
                    stage(u)
            for stage in (h_low, shift, choose, weigh):
                for u in first_units:
                    stage(u)

            def step(n, k, between=None):
                dve.wait_ge(w_turned, n + 1)
                dve.wait_ge(s_ready, n + 1)
                dve.wait_ge(t_ready, n)
                nc.vector.tensor_tensor(t1_sb[:], w_ps[:], s_sb[:], ALU.mult).then_inc(t1_ready, 1)
                dve.wait_ge(t1_ready, n + 1)
                dve.wait_ge(u_ready, n + 1)
                dve.wait_ge(t_hi_ready, n)
                dve.wait_ge(t_lo_ready, n)
                nc.vector.tensor_tensor(t_sb[:], u_ps[:], t1_sb[:], ALU.mult).then_inc(t_ready, 1)
                if between:
                    between()
                dve.wait_ge(t_hi_ready, n + 1)
                dve.wait_ge(down_done, n)
                nc.vector.tensor_tensor(t_lo[k % 2][:], t_sb[:], t_hi[k % 2][:].bitcast(F32), ALU.subtract).then_inc(t_lo_ready, 1)

            def turn(half, it, front, back):
                if front:
                    stats_x(front)
                beside = {0: [(h_low, back), (norm_x, front)], 1: [(shift, back), (exponents, front)],
                          2: [(choose, back), (states, front)], 3: [(mix, front)],
                          4: [(add_mixed, front), (weigh, back)]}
                for k in range(TURN_STEPS):
                    step(it * TURN_STEPS + (half * STEPS + k), k,
                         (lambda: norm_h(front)) if front and k == TURN_STEPS - 1 else None)
                    for stage, u in beside.get(k, []):
                        if u:
                            stage(u)

            LINKS = 22
            for half in range(2):
                if half == 0:
                    with dve.Fori(0, TURNS - 1) as it:
                        chain.enter(it, LINKS)
                        turn(half, it, later(it + 3), later(it + 2))
                    chain.leave(TURNS - 1)
                    turn(half, TURNS - 1, None, later(TURNS + 1))
                else:
                    with dve.Fori(0, TURNS) as it:
                        turn(half, it, None, None)
                dve.wait_ge(y_done, half + 1)
                if half:
                    dve.wait_ge(y_turned, half)
                nc.vector.tensor_copy(y_sb[:, 1, :], y_ps[1][:]).then_inc(y_copied, 1)
                dve.wait_ge(y_turned, half + 1)
                for t in range(HT):
                    at = half * HT + t
                    y = out_ps[t // 2][:, (t % 2) * C:(t % 2 + 1) * C].rearrange("p (k c) -> p c k", k=KT)
                    rows = x1[:, at, :].rearrange("p (c k) -> p c k", k=KT)
                    last = nc.vector.tensor_tensor(rows, rows, y, ALU.add)
                last.then_inc(out_ready, 1)


_INS = ['x', 'ctx_2048', 'L0_xattn_w', 'L0_xattn_u', 'L0_ffn_gate_w', 'L0_ffn_w_gate', 'L0_ffn_w_up', 'L0_ffn_w_down']
_OUTS = [((16, 64, 256), 'float32')]


def kernel(**inputs):
    import numpy as _np
    import concourse.bacc as _bacc
    from concourse import mybir as _mybir
    from concourse.bass_utils import run_bass_kernel_spmd as _run

    nc = _bacc.Bacc("TRN2", target_bir_lowering=False, num_devices=1)
    arrays, args = {}, []
    for name in _INS:
        a = _np.ascontiguousarray(inputs[name])
        arrays[f"in_{name}_dram"] = a
        args.append(nc.dram_tensor(f"in_{name}_dram", a.shape, _mybir.dt.from_np(a.dtype), kind="ExternalInput").ap())
    for i, (shape, dtype) in enumerate(_OUTS):
        dt = _mybir.dt.from_np(_np.dtype(dtype))
        args.append(nc.dram_tensor(f"out_{i}_dram", shape, dt, kind="ExternalOutput").ap())
    program(nc, *args)
    r = _run(nc, [arrays], core_ids=[0])
    got = tuple(r.results[0][f"out_{i}_dram"] for i in range(len(_OUTS)))
    return got[0]
```

```python
from contextlib import ExitStack

import concourse.bass as bass
from concourse import mybir

F32 = mybir.dt.float32
F32R = mybir.dt.float32r
BF16 = mybir.dt.bfloat16
ALU = mybir.AluOpType
ACT = mybir.ActivationFunctionType
AX = mybir.AxisListType

P = 128
TOP = 8
EPS = 1e-5
START_MAX = -1e38
RESET = -2e38
NO_WEIGHT = -1e4


class Chain:

    def __init__(self, engine, sem):
        self.engine, self.sem, self.count, self.turn = engine, sem, 0, None

    def add(self, instruction):
        self.count += 1
        instruction.then_inc(self.sem, 1)
        return self.count if self.turn is None else self.turn * self.per_turn + self.count

    def wait(self, value):
        self.engine.wait_ge(self.sem, value)

    def link(self, instruction):
        self.wait(self.add(instruction))

    def enter(self, turn, per_turn):
        self.turn, self.per_turn, self.entered = turn, per_turn, self.count

    def leave(self, turns):
        assert self.count - self.entered == self.per_turn, (self.count - self.entered, self.per_turn)
        self.count += (turns - 1) * self.per_turn
        self.turn = None


class Unit:

    def __init__(self, n, tile, tiles, slot, norms, capped):
        self.n, self.tile, self.tiles, self.slot = n, tile, tiles, slot
        self.first_norm, self.second_norm = norms or (None, None)
        self.capped = capped


def program(nc, x, ctx_in, decay, bonus, gate_w, w_gate, w_up, w_down, out):
    NB, S, C = x.shape
    E, _, INTER = w_gate.shape
    T = NB * S
    TILES = T // P
    HALF = T // 2
    HT = TILES // 2
    KT = C // P
    BPT = P // S
    NT = 2
    BK = NT * BPT * KT
    SP1 = S + 1
    CAP = 2 * (T * TOP // E)
    FT = E * INTER // P
    EG = 4
    GT = EG * INTER // P
    GF = EG * INTER
    GROUPS = E // EG
    assert GT * P == GF and CAP >= HALF and KT == 2 and GROUPS % 2 == 0
    PART = KT * GF
    assert PART == GT * C

    xt = x.rearrange("b s c -> (b s) c").rearrange("(n p) c -> p n c", p=P)
    ct = ctx_in.rearrange("b s c -> (b s) c").rearrange("(n p) c -> p n c", p=P)
    ot = out.rearrange("b s c -> (b s) c").rearrange("(n p) c -> p n c", p=P)
    wg_dram = w_gate.rearrange("e (p k) i -> p e (k i)", k=KT)
    wu_dram = w_up.rearrange("e (p k) i -> p e (k i)", k=KT)
    wd_dram = w_down.rearrange("e i c -> (e i) c").rearrange("(n p) c -> p n c", p=P)

    with ExitStack() as stack:
        def sb(name, shape, dt=F32):
            return stack.enter_context(nc.sbuf_tensor(name, shape, dt))

        def sem(name):
            return stack.enter_context(nc.semaphore(name))

        ident = sb("ident", [P, P])
        ident_bf = sb("ident_bf", [P, P], BF16)
        ones_bf = sb("ones_bf", [P, P], BF16)
        earlier = sb("earlier", [P, P], BF16)
        zeros_bf = sb("zeros_bf", [P, HALF], BF16)
        expert3 = sb("expert3", [3 * E, E], BF16)
        spread = sb("spread", [3 * E, E, INTER], BF16)
        table_in, table_out = sb("table_in", [P, 1]), sb("table_out", [P, 1])
        neg_half = sb("neg_half", [P, HT])
        decay_sb = sb("decay_sb", [P, KT])
        bonus_sb = sb("bonus_sb", [P, KT])
        decays = sb("decays", [P, BK, SP1])
        gate_sb = sb("gate_sb", [P, KT, E])
        gate_hi = sb("gate_hi", [P, KT, E], F32R)
        gate_lo = sb("gate_lo", [P, KT, E], F32R)
        x_sb = sb("x_sb", [P, TILES, C])
        ctx_sb = sb("ctx_sb", [P, HT, C])
        ctx_tile = sb("ctx_tile", [P, 1, C])
        x1 = sb("x1", [P, TILES, C])
        h_hi = sb("h_hi", [P, KT, T], F32R)
        h_lo = sb("h_lo", [P, KT, T], F32R)
        route = sb("route", [3 * E, T], BF16)
        counts = sb("counts", [P, E])
        def sets(name, shape, dt=F32):
            return [sb(f"{name}{i}", shape(n), dt) for i, n in enumerate((NT, NT, 1))]

        PAIRS = BPT * KT
        stats, mv = sets("stats", lambda n: [P, n, 6]), sets("mv", lambda n: [P, n, 2])
        var, rstd = sets("var", lambda n: [P, n]), sets("rstd", lambda n: [P, n])
        normed = sets("normed", lambda n: [P, n, C])
        kpad, vpad, opad, ev2 = (sets(name, lambda n: [P, n * PAIRS, SP1]) for name in ("kpad", "vpad", "opad", "ev2"))
        diffs = sets("diffs", lambda n: [P, 2, n * PAIRS, S])
        expo = sets("expo", lambda n: [P, 4, n * PAIRS, SP1])
        fact = expo[0:2] + [sb("fact2", [P, 4, PAIRS, SP1])]
        state = sets("state", lambda n: [P, 2, n * PAIRS, SP1])
        mixed = sets("mixed", lambda n: [P, KT * n * P])
        def route_sets(name, shape, dt=F32):
            return [sb(f"{name}{i}", shape(n), dt) for i, n in enumerate((HT, 1))]

        expd, replaced, rank, wts, rest = (
            route_sets(name, lambda n: [P, n, E]) for name in ("expd", "replaced", "rank", "wts", "rest"))
        top, neg_max = route_sets("top", lambda n: [P, n, TOP]), route_sets("neg_max", lambda n: [P, n])
        top_sum = route_sets("top_sum", lambda n: [P, 2, n])
        mask = route_sets("mask", lambda n: [P, n, E], BF16)
        parts = route_sets("parts", lambda n: [P, n, 3 * E], BF16)
        tile_hi = sb("tile_hi", [P, KT, P], F32R)
        tile_lo = sb("tile_lo", [P, KT, P], F32R)
        raw = [sb(f"raw{i}", [P, 3, PART]) for i in range(2)]
        whi = [sb(f"whi{i}", [P, 3, PART], F32R) for i in range(2)]
        wlo = [sb(f"wlo{i}", [P, 3, PART], F32R) for i in range(2)]
        s_sb = sb("s_sb", [P, HALF])
        t1_sb = sb("t1_sb", [P, HALF])
        t_sb = sb("t_sb", [P, HALF])
        t_hi = [sb(f"t_hi{i}", [P, HALF], F32R) for i in range(2)]
        t_lo = [sb(f"t_lo{i}", [P, HALF], F32R) for i in range(2)]
        y_sb = sb("y_sb", [P, KT, HALF])

        bank = [stack.enter_context(nc.psum_tensor(f"bank{i}", [P, 512], F32)) for i in range(8)]
        y_ps, g_ps, u_ps, w_ps = bank[0:2], (bank[2], bank[6]), bank[3], bank[4]

        k_ps = [bank[0], bank[2], bank[5]]
        mixed_ps = k_ps
        v_ps = [bank[1], bank[3], bank[5][:, 256:512]]
        h_ps = [bank[1], bank[3], bank[7]]
        logits_ps = [bank[4][:, 0:HT * E], bank[7][:, 256:256 + E]]
        ranks_ps = [bank[4][:, 0:(HT + 1) * E], bank[7][:, 288:288 + 2 * E]]
        parts_ps = [bank[4][:, 256:512].bitcast(BF16), bank[7][:, 384:384 + P // 2].bitcast(BF16)]
        out_ps = (bank[5], bank[7])

        x_landed = [sem(f"x_landed{i}") for i in range(3)]
        ctx_landed, tile_landed = sem("ctx_landed"), sem("tile_landed")
        small_landed, gate_landed = sem("small_landed"), sem("gate_landed")
        raw_landed = [sem(f"raw_landed{i}") for i in range(2)]
        out_stored = sem("out_stored")
        pool_chain, dve_chain, act_chain = sem("pool_chain"), sem("dve_chain"), sem("act_chain")
        consts_ready, settled, tables_ready = sem("consts_ready"), sem("settled"), sem("tables_ready")
        p_ready, num_ready = sem("p_ready"), sem("num_ready")
        silu_fetched = sem("silu_fetched")
        gate_hi_ready, gate_ready = sem("gate_hi_ready"), sem("gate_ready")
        var_ready, rstd_ready = sem("var_ready"), sem("rstd_ready")
        k_normed, k_turned, v_turned = sem("k_normed"), sem("k_turned"), sem("v_turned")
        k_ready, v_ready, steps_ready = sem("k_ready"), sem("v_ready"), sem("steps_ready")
        den_ready, inv_ready, e2v_ready = sem("den_ready"), sem("inv_ready"), sem("e2v_ready")
        expo_ready, fact_ready, mixed_ready, mixed_turned = sem("expo_ready"), sem("fact_ready"), sem("mixed_ready"), sem("mixed_turned")
        h_normed, h_turned, h_hi_ready, h_lo_ready = sem("h_normed"), sem("h_turned"), sem("h_hi_ready"), sem("h_lo_ready")
        logits_ready, max_ready, expd_ready = sem("logits_ready"), sem("max_ready"), sem("expd_ready")
        mask_ready, ranks_ready, parts_ready, parts_turned, route_ready = sem("mask_ready"), sem("ranks_ready"), sem("parts_ready"), sem("parts_turned"), sem("route_ready")
        ev_ready, h_lo_kept = sem("ev_ready"), sem("h_lo_kept")
        w_hi_ready, w_lo_ready = sem("w_hi_ready"), sem("w_lo_ready")
        w_turned, g_ready, u_ready, down_done = sem("w_turned"), sem("g_ready"), sem("u_ready"), sem("down_done")
        s_ready, t1_ready, t_ready, t_hi_ready, t_lo_ready = sem("s_ready"), sem("t1_ready"), sem("t_ready"), sem("t_hi_ready"), sem("t_lo_ready")
        y_copied = [sem(f"y_copied{k}") for k in range(KT)]
        y_turned, out_ready = sem("y_turned"), sem("out_ready")

        first_units = [Unit(n, NT * n, NT, n, (n, n + 3), False) for n in range(2)]
        LATER = HT

        def later(n):
            return Unit(n, n + 2, 1, 2, (n * 2, n * 2 + 1), True)

        early = Unit(2, HT, 1, 2, (2, 5), True)
        first_routed = Unit(0, 0, HT, 0, None, False)
        early_routed = Unit(1, HT, 1, 1, None, True)

        def later_routed(n):
            return Unit(n - 1, n + 2, 1, 1, None, True)

        ROUTED = 1 + LATER
        TURNS = GROUPS // 2
        STEPS = GROUPS * GT
        TURN_STEPS = 2 * GT

        def raw_parts(slot, part):
            r = raw[slot][:, part, :]
            if part < 2:
                return r.rearrange("p (e k i) -> p k e i", e=EG, k=KT)
            return r

        def split_view(w, slot, part):
            v = w[slot][:, part, :]
            if part < 2:
                return v.rearrange("p (k e i) -> p k e i", e=EG, k=KT)
            return v

        def up_weight(w, slot, part, k, j):
            at = k * GF + j * P
            return w[slot][:, part, at:at + P]

        def down_weight(w, slot, j, m):
            return w[slot][:, 2, j * C:(j + 1) * C].rearrange("p (c k) -> p k c", k=KT)[:, m, :]

        block = stack.enter_context(nc.Block())

        @block.sync
        def _(sp):
            sp.dma_start(x_sb[:, 0:1, :], xt[:, 0:1, :]).then_inc(x_landed[0], 16)
            sp.dma_start(x_sb[:, NT:2 * NT, :], xt[:, NT:2 * NT, :]).then_inc(x_landed[1], 16)
            sp.dma_start(x_sb[:, HT:, :], xt[:, HT:, :]).then_inc(x_landed[2], 16)

            def load(slot, group):
                experts = bass.ds(group * EG, EG)
                for part, w in ((0, wg_dram), (1, wu_dram)):
                    sp.dma_start(raw[slot][:, part, :].rearrange("p (e n) -> p e n", e=EG),
                                 w[:, experts, :]).then_inc(raw_landed[slot], 16)
                sp.dma_start(raw[slot][:, 2, :].rearrange("p (n c) -> p n c", n=GT),
                             wd_dram[:, bass.ds(group * GT, GT), :]).then_inc(raw_landed[slot], 16)

            sp.dma_start(ctx_tile[:], ct[:, HT:HT + 1, :]).then_inc(tile_landed, 16)
            load(0, 0)
            load(1, 1)
            def load_context(n):
                sp.wait_ge(v_turned, n)
                sp.dma_start(ctx_tile[:], ct[:, bass.ds(n + 2, 1), :]).then_inc(tile_landed, 16)

            def reload(half, slot, it, group):
                done = it * 6 + (half * GROUPS + slot + 1) * 3
                sp.wait_ge(w_hi_ready, done)
                sp.wait_ge(w_lo_ready, done)
                load(slot, group)

            for half in range(2):
                with sp.Fori(0, TURNS - 1) as it:
                    if half == 0:
                        load_context(it + 3)
                    for slot in range(2):
                        reload(half, slot, it, it * 2 + (2 + slot))
                if half == 0:
                    for slot in range(2):
                        reload(half, slot, TURNS - 1, slot)
            for quarter in range(4):
                sp.wait_ge(out_ready, quarter + 1)
                tiles = slice(quarter * NT, (quarter + 1) * NT)
                sp.dma_start(ot[:, tiles, :], x1[:, tiles, :]).then_inc(out_stored, 16)
            sp.wait_ge(out_stored, 64)

        @block.gpsimd
        def _(pool):
            pool.sem_inc(t_lo_ready, 1)
            chain = Chain(pool, pool_chain)
            pool.memset(ident[:], 0.0)
            pool.memset(ident_bf[:], 0.0)
            pool.memset(expert3[:], 0.0)
            pool.memset(zeros_bf[:], 0.0)
            pool.memset(ones_bf[:], 1.0)
            chain.link(pool.memset(earlier[:], 1.0))
            pool.affine_select(out=ident[:], in_=ident[:], compare_op=ALU.not_equal, fill=1.0, base=0,
                               pattern=[[-1, P]], channel_multiplier=1).then_inc(consts_ready, 1)
            pool.affine_select(out=ident_bf[:], in_=ident_bf[:], compare_op=ALU.not_equal, fill=1.0, base=0,
                               pattern=[[-1, P]], channel_multiplier=1)
            pool.affine_select(out=earlier[:], in_=earlier[:], compare_op=ALU.is_gt, fill=0.0, base=0,
                               pattern=[[1, P]], channel_multiplier=-1)
            for part in range(3):
                chain.link(pool.affine_select(out=expert3[:], in_=expert3[:], compare_op=ALU.not_equal, fill=1.0,
                                              base=-part * E, pattern=[[-1, E]], channel_multiplier=1))
            pool.memset(neg_half[:], -0.5).then_inc(consts_ready, 1)

            def split_low(slot, part, group):
                pool.wait_ge(w_hi_ready, group * 3 + part + 1)
                if not isinstance(group, int) or group >= 2:
                    pool.wait_ge(down_done, (group - 1) * GT + 2)
                pool.tensor_tensor(split_view(wlo, slot, part), raw_parts(slot, part),
                                   split_view(whi, slot, part).bitcast(F32), ALU.subtract).then_inc(w_lo_ready, 1)

            pool.wait_ge(consts_ready, 2)
            def power(u, norm):
                pool.wait_ge(var_ready, norm + 1)
                pool.tensor_tensor(rstd[u.slot][:], var[u.slot][:], neg_half[:, 0:u.tiles], ALU.pow).then_inc(rstd_ready, 1)

            def state_values(u):
                pool.wait_ge(v_ready, u.n + 1)
                pool.wait_ge(steps_ready, u.n + 1)
                pool.tensor_tensor(ev2[u.slot][:], fact[u.slot][:, 3], vpad[u.slot][:], ALU.mult).then_inc(e2v_ready, 1)

            def numerators(u):
                pool.wait_ge(p_ready, u.n + 1)
                num = diffs[u.slot][:, 0]
                chain.link(pool.tensor_tensor(num, fact[u.slot][:, 2, :, 1:], state[u.slot][:, 0, :, 0:S], ALU.mult))
                pool.tensor_tensor(num, num, opad[u.slot][:, :, 1:], ALU.add).then_inc(num_ready, 1)

            def new_values(u):
                pool.wait_ge(fact_ready, u.n + 1)
                pool.tensor_tensor(opad[u.slot][:, :, 1:], fact[u.slot][:, 0, :, 1:], vpad[u.slot][:, :, 1:],
                                   ALU.mult).then_inc(ev_ready, 1)

            def keep_low(u):
                pool.wait_ge(h_lo_ready, u.n + 1)
                pool.tensor_copy(h_lo[:, :, bass.ds(u.tile * P, P)], tile_lo[:].bitcast(F32)).then_inc(h_lo_kept, 1)

            for u in (*first_units, early):
                power(u, u.first_norm)
            for u in first_units:
                state_values(u)
                new_values(u)
            for u in first_units:
                numerators(u)
            for part in range(2):
                split_low(0, part, 0)
            for u in first_units:
                power(u, u.second_norm)
            state_values(early)
            new_values(early)
            split_low(0, 2, 0)
            power(early, early.second_norm)

            def product_low(n, k):
                pool.wait_ge(t_hi_ready, n + 2)
                pool.wait_ge(down_done, n + 1)
                pool.tensor_tensor(t_lo[k % 2][:], t_sb[:], t_hi[k % 2][:].bitcast(F32), ALU.subtract).then_inc(t_lo_ready, 1)

            def turn(half, it, front, back, final=False):
                for k in range(TURN_STEPS):
                    if not final or k < TURN_STEPS - 1:
                        product_low(it * TURN_STEPS + (half * STEPS + k), k)
                    if front and k == 0:
                        power(front, front.first_norm)
                    if front and k == 5:
                        power(front, front.second_norm)
                    ahead = k // GT + 1
                    if ahead == 1 or not final:
                        split_low(ahead % 2, k % GT, it * 2 + (half * GROUPS + ahead))
                    if back and k == 0:
                        keep_low(back)
                    if front and k == 2:
                        state_values(front)
                        new_values(front)

            with pool.Fori(0, TURNS - 1) as it:
                turn(0, it, later(it + 3), later(it + 2))
            turn(0, TURNS - 1, None, later(TURNS + 1))
            with pool.Fori(0, TURNS - 1) as it:
                turn(1, it, None, None)
            turn(1, TURNS - 1, None, None, final=True)

        @block.scalar
        def _(act):
            act.dma_start(x_sb[:, 1:NT, :], xt[:, 1:NT, :]).then_inc(x_landed[0], 16)
            act.dma_start(decay_sb[:], decay.rearrange("(p k) -> p k", k=KT)).then_inc(small_landed, 16)
            act.dma_start(bonus_sb[:], bonus.rearrange("(p k) -> p k", k=KT)).then_inc(small_landed, 16)
            act.dma_start(ctx_sb[:], ct[:, 0:HT, :]).then_inc(ctx_landed, 16)
            act.dma_start(gate_sb[:], gate_w.rearrange("(p k) e -> p k e", k=KT)).then_inc(gate_landed, 16)

            act.sem_inc(t_hi_ready, 1)
            act.sem_inc(silu_fetched, 1)
            chain = Chain(act, act_chain)

            def take(u, turned, at, pad, ready):
                act.wait_ge(turned, u.n + 1)
                to = pad[u.slot][:, :, 1:].rearrange("p (b k) s -> p k b s", k=KT)
                fr = at[u.slot][:, 0:KT * u.tiles * P].rearrange("p (k b s) -> p k b s", k=KT, s=S)
                nc.scalar.activation(to, fr, ACT.Copy).then_inc(ready, 1)

            def take_k(u):
                take(u, k_turned if u.slot < 2 else v_turned, k_ps, kpad, k_ready)

            def take_v(u):
                take(u, v_turned, v_ps, vpad, v_ready)

            def exps(u):
                for pair, ready in ((1, steps_ready), (0, fact_ready)):
                    sign = 1.0
                    if u.slot < 2:
                        act.wait_ge(expo_ready, u.n * 2 + 2 - pair)
                        if pair == 0:
                            sign = -1.0
                            nc.scalar.activation(expo[u.slot][:, 0, :, 1:], diffs[u.slot][:, 0], ACT.Relu, scale=-1.0)
                            chain.link(nc.scalar.activation(expo[u.slot][:, 2, :, 1:], diffs[u.slot][:, 0], ACT.Relu))
                    elif pair:
                        act.wait_ge(expo_ready, u.n + 3)
                    nc.scalar.activation(fact[u.slot][:, pair::2], expo[u.slot][:, pair::2], ACT.Exp, scale=sign).then_inc(ready, 1)

            def invert():
                for u in first_units:
                    act.wait_ge(den_ready, u.n + 1)
                    last = nc.scalar.activation(kpad[u.slot][:, :, 1:], diffs[u.slot][:, 1], ACT.Ln)
                chain.link(last)
                for u in first_units:
                    inv = kpad[u.slot][:, :, 1:]
                    nc.scalar.activation(inv, inv, ACT.Exp, scale=-1.0).then_inc(inv_ready, 1)

            def spread_experts():
                act.wait_ge(consts_ready, 2)
                nc.scalar.activation(spread[:], expert3[:, :, None].to_broadcast([3 * E, E, INTER]), ACT.Copy).then_inc(tables_ready, 1)

            def take_h(u):
                act.wait_ge(h_turned, u.n + 1)
                cols = u.tiles * P
                fr = h_ps[u.slot][:, 0:KT * cols].rearrange("p (k t) -> p k t", k=KT)
                if u.slot < 2:
                    at = u.tile * P
                    nc.scalar.activation(h_hi[:, :, at:at + cols], fr, ACT.Copy).then_inc(h_hi_ready, 1)
                else:
                    nc.scalar.activation(tile_hi[:], fr, ACT.Copy).then_inc(h_hi_ready, 1)
                    act.wait_ge(h_hi_ready, u.n + 1)
                    nc.scalar.activation(h_hi[:, :, bass.ds(u.tile * P, P)], tile_hi[:].bitcast(F32), ACT.Copy)

            def route_exps(u):
                act.wait_ge(max_ready, u.n + 1)
                for t in range(u.tiles):
                    last = nc.scalar.activation(expd[u.slot][:, t, :], logits_ps[u.slot][:, t * E:(t + 1) * E], ACT.Exp,
                                                bias=neg_max[u.slot][:, t:t + 1])
                last.then_inc(expd_ready, 1)

            def take_route(u):
                act.wait_ge(parts_turned, u.n + 1)
                cols = u.tiles * P
                fr = parts_ps[u.slot][0:3 * E, 0:cols]
                nc.scalar.activation(route[:, bass.ds(u.tile * P, cols)], fr, ACT.Copy).then_inc(route_ready, 1)

            def fetch_silu(n):
                act.wait_ge(silu_fetched, n + 1)
                nc.scalar.activation(table_out[:], table_in[:], ACT.Silu).then_inc(silu_fetched, 1)

            def split_high(slot, part, group):
                act.wait_ge(raw_landed[slot], group * 24 + (48 - slot * 24))
                if not isinstance(group, int) or group >= 2:
                    act.wait_ge(down_done, (group - 1) * GT + 2)
                nc.scalar.activation(split_view(whi, slot, part), raw_parts(slot, part), ACT.Copy).then_inc(w_hi_ready, 1)

            for stage in (take_k, take_v):
                for u in first_units:
                    stage(u)
            act.wait_ge(gate_landed, 16)
            nc.scalar.activation(gate_hi[:], gate_sb[:], ACT.Copy).then_inc(gate_hi_ready, 1)
            exps(first_units[0])
            exps(first_units[1])
            take_k(early)
            take_v(early)
            invert()
            for part in range(3):
                split_high(0, part, 0)
            exps(early)
            spread_experts()
            for u in first_units:
                take_h(u)
            route_exps(first_routed)

            def step(n, k, between=None):
                act.wait_ge(g_ready, n + 1)
                act.wait_ge(t1_ready, n + 1)
                nc.scalar.activation(s_sb[:], g_ps[k % 2][:], ACT.Silu).then_inc(s_ready, 1)
                if between:
                    between()
                act.wait_ge(t_ready, n + 2)
                act.wait_ge(down_done, n + 1)
                nc.scalar.activation(t_hi[k % 2][:], t_sb[:], ACT.Copy).then_inc(t_hi_ready, 1)

            def turn(half, it, front, back, routed, first_turn=False, final=False):
                def all_exps():
                    if back:
                        route_exps(routed)
                    if front:
                        exps(front)
                    fetch_silu(it * 2)

                beside = {2: all_exps}
                if first_turn:
                    beside[0] = lambda: take_route(first_routed)
                    beside[1] = lambda: take_h(back)
                if half == 0 and not first_turn:
                    fetch_silu(it * 2 - 1)
                for k in range(TURN_STEPS):
                    step(it * TURN_STEPS + (half * STEPS + k), k, beside.get(k) if half == 0 else None)
                    if back and k == 0 and not first_turn:
                        take_h(back)
                    if front and k == 1:
                        take_k(front)
                        take_v(front)
                    ahead = k // GT + 1
                    if ahead == 1 or not final:
                        split_high(ahead % 2, k % GT, it * 2 + (half * GROUPS + ahead))
                    if back and k == TURN_STEPS - 1:
                        take_route(routed)

            def take_y(half):
                act.wait_ge(down_done, (half + 1) * STEPS + 2)
                if half:
                    act.wait_ge(y_turned, 2)
                for q in range(2):
                    cols = slice(q * NT * P, (q + 1) * NT * P)
                    nc.scalar.activation(y_sb[:, 0, cols], y_ps[0][:, cols], ACT.Copy).then_inc(y_copied[0], 1)

            turn(0, 0, later(3), later(2), later_routed(2), first_turn=True)
            with act.Fori(1, TURNS - 1) as it:
                turn(0, it, later(it + 3), later(it + 2), later_routed(it + 2))
            turn(0, TURNS - 1, None, later(TURNS + 1), later_routed(TURNS + 1))
            take_y(0)
            with act.Fori(0, TURNS - 1) as it:
                turn(1, it, None, None, None)
            turn(1, TURNS - 1, None, None, None, final=True)
            take_y(1)

        @block.tensor
        def _(pe):
            def turn_kv(u):
                if u is first_units[0]:
                    pe.wait_ge(consts_ready, 1)
                pe.wait_ge(k_normed, u.n + 1)
                if u.slot < 2:
                    context = ctx_sb[:, u.tile:u.tile + u.tiles, :]
                else:
                    pe.wait_ge(tile_landed, (u.n - 1) * 16)
                    if u is not early:
                        pe.wait_ge(h_normed, u.n)
                    context = ctx_tile[:]
                for to, src, turned in ((k_ps[u.slot], normed[u.slot][:], k_turned), (v_ps[u.slot], context, v_turned)):
                    if turned is v_turned and u.slot < 2:
                        pe.wait_ge(ctx_landed, 16)
                    for t in range(u.tiles):
                        rows = src[:, t, :].rearrange("p (c k) -> p k c", k=KT)
                        for k in range(KT):
                            at = (k * u.tiles + t) * P
                            last = nc.tensor.transpose(to[:, at:at + P], rows[:, k, :], ident[:])
                    last.then_inc(turned, 1)

            def turn_mixed(u):
                pe.wait_ge(mixed_ready, u.n + 1)
                for t in range(u.tiles):
                    for k in range(KT):
                        at = (t * KT + k) * P
                        last = nc.tensor.transpose(mixed_ps[u.slot][:, at:at + P],
                                                   mixed[u.slot][:, (k * u.tiles + t) * P:(k * u.tiles + t + 1) * P], ident[:])
                last.then_inc(mixed_turned, 1)

            def turn_h(u):
                pe.wait_ge(h_normed, u.n + 1)
                if u.slot == 2:
                    pe.wait_ge(route_ready, u.n - 1)
                for t in range(u.tiles):
                    rows = normed[u.slot][:, t, :].rearrange("p (c k) -> p k c", k=KT)
                    for k in range(KT):
                        at = (k * u.tiles + t) * P
                        last = nc.tensor.transpose(h_ps[u.slot][:, at:at + P], rows[:, k, :], ident[:])
                last.then_inc(h_turned, 1)

            def logits(u):
                if u is first_routed:
                    pe.wait_ge(gate_ready, 1)
                for t in range(u.tiles):
                    if t % NT == 0:
                        pe.wait_ge(h_hi_ready, u.n + (t // NT + 1 if u is first_routed else 2))
                        pe.wait_ge(h_lo_ready, u.n + (t // NT + 1 if u is first_routed else 2))
                    if u is first_routed:
                        cols = slice((u.tile + t) * P, (u.tile + t + 1) * P)
                        hi, lo = h_hi[:, :, cols], h_lo[:, :, cols]
                    else:
                        hi, lo = tile_hi[:], tile_lo[:]
                    terms = [(a, b, k) for k in range(KT) for a, b in ((hi, gate_hi), (hi, gate_lo), (lo, gate_hi))]
                    for n, (a, b, k) in enumerate(terms):
                        last = nc.tensor.matmul(logits_ps[u.slot][:, t * E:(t + 1) * E], a[:, k, :], b[:, k, :],
                                                start=(n == 0), stop=(n == len(terms) - 1))
                last.then_inc(logits_ready, 1)

            def ranks(u):
                pe.wait_ge(mask_ready, u.n + 1)
                if u is first_routed:
                    pe.wait_ge(consts_ready, 2)
                to = ranks_ps[u.slot]
                if u.capped:
                    for t in range(u.tiles):
                        for s in range(t + 1):
                            nc.tensor.matmul(to[:, t * E:(t + 1) * E], (earlier if s == t else ones_bf)[:], mask[u.slot][:, s, :],
                                             start=(s == 0), stop=(s == t))
                for s in range(u.tiles):
                    last = nc.tensor.matmul(to[:, u.tiles * E:(u.tiles + 1) * E], ones_bf[:], mask[u.slot][:, s, :],
                                            start=(s == 0), stop=(s == u.tiles - 1))
                last.then_inc(ranks_ready, 1)

            def turn_parts(u):
                pe.wait_ge(parts_ready, u.n + 1)
                to = parts_ps[u.slot]
                for t in range(u.tiles):
                    last = nc.tensor.transpose(to[0:3 * E, t * P:(t + 1) * P], parts[u.slot][:, t, :], ident_bf[:])
                last.then_inc(parts_turned, 1)

            def project(n, half, part, slot, j, odd, group):
                tokens = slice(half * HALF, (half + 1) * HALF)
                ps, ready = ((g_ps[odd], g_ready), (u_ps, u_ready))[part]
                if part == 1:
                    pe.wait_ge(t_ready, n + 1)
                elif not isinstance(n, int) or n >= 2:
                    pe.wait_ge(s_ready, n - 1)
                if j == 0:
                    pe.wait_ge(w_hi_ready, group * 3 + (part + 1))
                    pe.wait_ge(w_lo_ready, group * 3 + (part + 1))
                terms = [(w, h, k) for k in range(KT) for w, h in ((whi, h_hi), (whi, h_lo), (wlo, h_hi))]
                for i, (w, h, k) in enumerate(terms):
                    last = nc.tensor.matmul(ps[:], up_weight(w, slot, part, k, j), h[:, k, tokens],
                                            start=(i == 0), stop=(i == len(terms) - 1))
                last.then_inc(ready, 1)

            def weights(n, half, tile):
                pe.wait_ge(t1_ready, n + 1)
                nc.tensor.matmul(w_ps[:], spread[:].rearrange("p e i -> p (e i)")[:, bass.ds(tile * P, P)],
                                 route[:, half * HALF:(half + 1) * HALF], start=True, stop=True).then_inc(w_turned, 1)

            def down(n, slot, j, odd, group, last_step=False):
                if j == 0:
                    pe.wait_ge(w_hi_ready, group * 3 + 3)
                    pe.wait_ge(w_lo_ready, group * 3 + 3)
                pe.wait_ge(t_hi_ready, n + 2)
                for m in range(KT):
                    nc.tensor.matmul(y_ps[m][:], down_weight(whi, slot, j, m), t_hi[odd][:], start=False, stop=False)
                    nc.tensor.matmul(y_ps[m][:], down_weight(wlo, slot, j, m), t_hi[odd][:], start=False, stop=False)
                pe.wait_ge(t_lo_ready, n + 2)
                for m in range(KT):
                    last = nc.tensor.matmul(y_ps[m][:], down_weight(whi, slot, j, m), t_lo[odd][:],
                                            start=False, stop=last_step)
                last.then_inc(down_done, 1)

            def keep_clock(count):
                for i in range(count):
                    nc.tensor.matmul(bank[7][:], zeros_bf[:, 0:P], zeros_bf[:], start=(i == 0), stop=(i == count - 1))

            def start_sums():
                for m in range(KT):
                    nc.tensor.matmul(y_ps[m][:], zeros_bf[:, 0:P], zeros_bf[:], start=True, stop=False)

            def turn_output(half):
                if half:
                    pe.wait_ge(out_ready, 2)
                for q in range(2):
                    for k in range(KT):
                        pe.wait_ge(y_copied[k], half * 2 + q + 1)
                    for t in range(NT):
                        for k in range(KT):
                            at, token = (t * KT + k) * P, (q * NT + t) * P
                            last = nc.tensor.transpose(out_ps[q][:, at:at + P], y_sb[:, k, token:token + P], ident[:])
                    last.then_inc(y_turned, 1)

            def turn(half, it, front, back, routed, first_turn=False, last_turn=False):
                for k in range(TURN_STEPS):
                    n = it * TURN_STEPS + (half * STEPS + k)
                    slot, j = k // GT, k % GT
                    final = half == 1 and last_turn and k == TURN_STEPS - 1
                    if final:
                        weights(n, half, it * TURN_STEPS + k)
                    if half or not first_turn or k:
                        project(n, half, 1, slot, j, k % 2, it * 2 + (half * GROUPS + slot))
                    if back and first_turn and k == 1:
                        project(n + 1, half, 0, 0, 2, 0, 0)
                        turn_h(back)
                    if first_turn and k == 0:
                        pe.wait_ge(route_ready, ROUTED if half else 1)
                        if half == 0:
                            pe.wait_ge(tables_ready, 1)
                    if not final:
                        weights(n, half, it * TURN_STEPS + k)
                    if front and k == 1:
                        turn_kv(front)
                    if back and k == 1:
                        logits(routed)
                    if back and k == 3:
                        ranks(routed)
                    if front and k == 5:
                        turn_mixed(front)
                    if back and k == 5:
                        turn_parts(routed)
                    if half == 0 and first_turn and k == 0:
                        keep_clock(5)
                    elif half == 0 and first_turn and k == 1:
                        pass
                    elif k < TURN_STEPS - 1 or not last_turn:
                        project(n + 1, half, 0, (k + 1) // GT % 2, (k + 1) % GT, (k + 1) % 2,
                                it * 2 + (half * GROUPS + (k + 1) // GT))
                    elif half == 0:
                        pe.wait_ge(h_lo_kept, LATER)
                        project(n + 1, 1, 0, 0, 0, 0, GROUPS)
                    if k > 0:
                        down(n - 1, (k - 1) // GT, (k - 1) % GT, (k - 1) % 2, it * 2 + (half * GROUPS + (k - 1) // GT))
                    elif not first_turn:
                        down(n - 1, 1, GT - 1, 1, None)
                    else:
                        if half:
                            turn_output(0)
                        start_sums()
                    if back and k == 0 and not first_turn:
                        turn_h(back)

            pe.sem_inc(down_done, 2)
            pe.wait_ge(consts_ready, 1)
            keep_clock(10)
            for u in (*first_units, early):
                turn_kv(u)
            pe.wait_ge(inv_ready, 1)
            keep_clock(7)
            turn_mixed(first_units[0])
            turn_mixed(first_units[1])
            keep_clock(26)
            turn_h(first_units[0])
            turn_h(first_units[1])
            keep_clock(5)
            logits(first_routed)
            project(0, 0, 0, 0, 0, 0, 0)
            project(0, 0, 1, 0, 0, 0, 0)
            ranks(first_routed)
            project(1, 0, 0, 0, 1, 1, 0)
            turn_parts(first_routed)
            turn_mixed(early)
            turn(0, 0, later(3), later(2), later_routed(2), first_turn=True)
            with pe.Fori(1, TURNS - 1) as it:
                turn(0, it, later(it + 3), later(it + 2), later_routed(it + 2))
            turn(0, TURNS - 1, None, later(TURNS + 1), later_routed(TURNS + 1), last_turn=True)
            down(STEPS - 1, 1, GT - 1, 1, None, last_step=True)
            turn(1, 0, None, None, None, first_turn=True)
            with pe.Fori(1, TURNS - 1) as it:
                turn(1, it, None, None, None)
            turn(1, TURNS - 1, None, None, None, last_turn=True)
            down(2 * STEPS - 1, 1, GT - 1, 1, None, last_step=True)
            turn_output(1)

        @block.vector
        def _(dve):
            dve.sem_inc(t1_ready, 1)
            dve.sem_inc(t_ready, 1)
            chain = Chain(dve, dve_chain)
            link = chain.link
            for s in range(3):
                nc.vector.memset(kpad[s][:, :, 0:1], START_MAX)
                nc.vector.memset(vpad[s][:, :, 0:1], 0.0)
                for q in range(4):
                    nc.vector.memset(expo[s][:, q, :, 0:1], -NO_WEIGHT if s < 2 and q % 2 == 0 else NO_WEIGHT)
            nc.vector.memset(counts[:], 0.0)
            nc.vector.memset(table_in[:], 0.0)
            link(nc.vector.memset(decays[:], 0.0))

            def settle():
                dve.sem_inc(settled, 1)

            def link_settled(instruction):
                chain.link(instruction)
                settle()

            def norm_stats(src, *units):
                for u in units:
                    for t in range(u.tiles):
                        last = nc.vector.bn_stats(stats[u.slot][:, t, :], src[:, u.tile + t, :])
                link_settled(last)
                for u in units:
                    for t in range(u.tiles):
                        last = nc.vector.bn_aggr(mv[u.slot][:, t, :], stats[u.slot][:, t, :])
                link(last)
                for u in units:
                    nc.vector.tensor_scalar(var[u.slot][:], mv[u.slot][:, :, 1], EPS, None, ALU.add).then_inc(var_ready, 1)

            def norm_apply(u, src, ready, norm):
                dve.wait_ge(rstd_ready, norm + 1)
                for t in range(u.tiles):
                    last = nc.vector.tensor_scalar(normed[u.slot][:, t, :], src[:, u.tile + t, :], mv[u.slot][:, t, 0:1],
                                                   rstd[u.slot][:, t:t + 1], ALU.subtract, ALU.mult)
                last.then_inc(ready, 1)

            def stats_x(u):
                dve.wait_ge(x_landed[u.slot], 32 if u.slot == 0 else 16)
                norm_stats(x_sb, u)

            def norm_x(u):
                norm_apply(u, x_sb, k_normed, u.first_norm)

            def tables():
                dve.wait_ge(small_landed, 32)
                by = decays[:].rearrange("p (b k) s -> p b k s", k=KT)
                for k in range(KT):
                    nc.vector.tensor_scalar(by[:, :, k, 1:], by[:, :, k, 1:], decay_sb[:, k:k + 1], None, ALU.add)
                link(nc.vector.memset(decays[:, :, 0:1], RESET))

            def flat(a):
                return a.rearrange("p b s -> p (b s)")

            def clamp(u, pair):
                first, second = slice(pair.start, pair.stop), slice(pair.start + 2, pair.stop + 2)
                nc.vector.tensor_scalar(expo[u.slot][:, first, :, 1:], diffs[u.slot][:, pair], 0.0, None, ALU.min)
                nc.vector.tensor_scalar(expo[u.slot][:, second, :, 1:], diffs[u.slot][:, pair], -1.0, 0.0,
                                        ALU.mult, ALU.min).then_inc(expo_ready, 1)

            def exponents(u, clamped=True):
                dve.wait_ge(k_ready, u.n + 1)
                bk = u.tiles * BPT * KT
                k_, o_ = kpad[u.slot][:], opad[u.slot][:]
                link(nc.vector.tensor_tensor_scan(flat(o_), flat(decays[:, 0:bk, :]), flat(k_), 0.0, ALU.add, ALU.max))
                for pair in (1, 0):
                    for k in range(KT):
                        now = k_.rearrange("p (b k) s -> p b k s", k=KT)[:, :, k, 1:]
                        was = o_.rearrange("p (b k) s -> p b k s", k=KT)[:, :, k, 0:S]
                        d = diffs[u.slot][:, pair].rearrange("p (b k) s -> p b k s", k=KT)[:, :, k, :]
                        if pair:
                            last = nc.vector.scalar_tensor_tensor(out=d, in0=was, scalar=decay_sb[:, k:k + 1], in1=now,
                                                                  op0=ALU.add, op1=ALU.subtract)
                        else:
                            last = nc.vector.scalar_tensor_tensor(out=d, in0=now, scalar=bonus_sb[:, k:k + 1], in1=was,
                                                                  op0=ALU.add, op1=ALU.subtract)
                    if u.slot == 2:
                        continue
                    if pair:
                        link(last)
                        clamp(u, slice(1, 2))
                    else:
                        last.then_inc(expo_ready, 1)
                if u.slot == 2 and not clamped:
                    return chain.add(last)
                if u.slot == 2:
                    link(last)
                    clamp(u, slice(0, 2))

            def state_q(*units):
                done = []
                for u in units:
                    dve.wait_ge(steps_ready, u.n + 1)
                    done.append(chain.add(nc.vector.tensor_tensor_scan(
                        flat(state[u.slot][:, 1]), flat(fact[u.slot][:, 1]), flat(fact[u.slot][:, 3]), 0.0, ALU.mult, ALU.add)))
                for i, u in enumerate(units):
                    dve.wait_ge(fact_ready, u.n + 1)
                    chain.wait(done[i])
                    done[i] = chain.add(nc.vector.tensor_tensor(diffs[u.slot][:, 1], fact[u.slot][:, 2, :, 1:],
                                                                state[u.slot][:, 1, :, 0:S], ALU.mult))
                for i, u in enumerate(units):
                    den = diffs[u.slot][:, 1]
                    chain.wait(done[i])
                    last = nc.vector.tensor_tensor(den, den, fact[u.slot][:, 0, :, 1:], ALU.add)
                    if u.slot < 2:
                        last.then_inc(den_ready, 1)
                    else:
                        link(last)

            def invert(u):
                nc.vector.reciprocal(diffs[u.slot][:, 1], diffs[u.slot][:, 1])

            def state_p(u):
                _, a2, a, _ = (fact[u.slot][:, q] for q in range(4))
                num = diffs[u.slot][:, 0]
                dve.wait_ge(e2v_ready, u.n + 1)
                scan = nc.vector.tensor_tensor_scan(flat(state[u.slot][:, 0]), flat(a2), flat(ev2[u.slot][:]), 0.0, ALU.mult, ALU.add)
                if u.slot < 2:
                    scan.then_inc(p_ready, 1)
                    return
                link(scan)
                link(nc.vector.tensor_tensor(num, a[:, :, 1:], state[u.slot][:, 0, :, 0:S], ALU.mult))

            def mix(*units):
                done = []
                for u in units:
                    num, den = (diffs[u.slot][:, q] for q in range(2))
                    if u.slot == 2:
                        dve.wait_ge(ev_ready, u.n + 1)
                        done.append(chain.add(nc.vector.tensor_tensor(num, num, opad[u.slot][:, :, 1:], ALU.add)))
                    else:
                        dve.wait_ge(p_ready, u.n + 1)
                        dve.wait_ge(inv_ready, u.n + 1)
                        done.append(chain.add(nc.vector.tensor_tensor(ev2[u.slot][:, :, 1:], den, kpad[u.slot][:, :, 1:], ALU.mult)))
                for i, u in enumerate(units):
                    if u.slot < 2:
                        chain.wait(done[i])
                        done[i] = chain.add(nc.vector.scalar_tensor_tensor(
                            out=diffs[u.slot][:, 1], in0=ev2[u.slot][:, :, 1:], scalar=2.0, in1=kpad[u.slot][:, :, 1:],
                            op0=ALU.subtract, op1=ALU.mult))
                by_token = lambda v: v.rearrange("p (b k) s -> p b k s", k=KT)
                for i, u in enumerate(units):
                    num, den = (diffs[u.slot][:, q] for q in range(2))
                    y = mixed[u.slot][:].rearrange("p (k b s) -> p b k s", k=KT, s=S)
                    if u.slot < 2:
                        dve.wait_ge(num_ready, u.n + 1)
                    chain.wait(done[i])
                    nc.vector.tensor_tensor(y, by_token(num), by_token(den), ALU.mult).then_inc(mixed_ready, 1)

            def add_mixed(*units):
                for u in units:
                    dve.wait_ge(mixed_turned, u.n + 1)
                    for t in range(u.tiles):
                        y = mixed_ps[u.slot][:, t * C:(t + 1) * C].rearrange("p (k c) -> p c k", k=KT)
                        last = nc.vector.tensor_tensor(x1[:, u.tile + t, :].rearrange("p (c k) -> p c k", k=KT),
                                                       x_sb[:, u.tile + t, :].rearrange("p (c k) -> p c k", k=KT), y,
                                                       ALU.subtract if u.slot < 2 else ALU.add)
                link_settled(last)
                norm_stats(x1, *units)

            def norm_h(u):
                norm_apply(u, x1, h_normed, u.second_norm)

            def h_low(u):
                dve.wait_ge(h_hi_ready, u.n + 1)
                cols = slice(u.tile * P, (u.tile + u.tiles) * P) if u.slot < 2 else None
                fr = h_ps[u.slot][:, 0:KT * u.tiles * P].rearrange("p (k t) -> p k t", k=KT)
                hi, lo = (h_hi[:, :, cols], h_lo[:, :, cols]) if u.slot < 2 else (tile_hi[:], tile_lo[:])
                nc.vector.tensor_tensor(lo, fr, hi.bitcast(F32), ALU.subtract).then_inc(h_lo_ready, 1)

            def largest(u):
                dve.wait_ge(logits_ready, u.n + 1)
                n = slice(0, u.tiles)
                lg = logits_ps[u.slot][:, 0:u.tiles * E].rearrange("p (n e) -> p n e", e=E)
                nc.vector.tensor_reduce(neg_max[u.slot][:, n], lg, AX.X, ALU.max, negate=True).then_inc(max_ready, 1)

            def choose(u):
                dve.wait_ge(expd_ready, u.n + 1)
                settle()
                n = slice(0, u.tiles)
                for t in range(u.tiles):
                    last = nc.vector.max(top[u.slot][:, t, :], expd[u.slot][:, t, :])
                link_settled(last)
                for t in range(u.tiles):
                    nc.vector.match_replace(out=replaced[u.slot][:, t, :], in_to_replace=top[u.slot][:, t, :],
                                            in_values=expd[u.slot][:, t, :], imm_value=-1.0)
                link(nc.vector.reduce_sum(top_sum[u.slot][:, 0, n], top[u.slot][:, n, :], AX.X))
                nc.vector.reciprocal(top_sum[u.slot][:, 1, n], top_sum[u.slot][:, 0, n])
                nc.vector.tensor_scalar(mask[u.slot][:, n, :], replaced[u.slot][:, n, :], 0.0, None, ALU.is_lt).then_inc(mask_ready, 1)
                dve.wait_ge(mask_ready, u.n + 1)
                for t in range(u.tiles):
                    last = nc.vector.scalar_tensor_tensor(out=wts[u.slot][:, t, :], in0=expd[u.slot][:, t, :],
                                                          scalar=top_sum[u.slot][:, 1, t:t + 1], in1=mask[u.slot][:, t, :],
                                                          op0=ALU.mult, op1=ALU.mult)
                link(last)

            def weigh(u):
                s, n = u.slot, slice(0, u.tiles)

                def count():
                    dve.wait_ge(ranks_ready, u.n + 1)
                    link(nc.vector.tensor_tensor(counts[:], counts[:], ranks_ps[s][:, u.tiles * E:(u.tiles + 1) * E], ALU.add))

                if u.capped:
                    dve.wait_ge(ranks_ready, u.n + 1)
                    for t in range(u.tiles):
                        last = nc.vector.tensor_tensor(rank[s][:, t, :], ranks_ps[s][:, t * E:(t + 1) * E], counts[:], ALU.add)
                    link(last)
                    link(nc.vector.scalar_tensor_tensor(out=wts[s][:, n, :], in0=rank[s][:, n, :], scalar=float(CAP),
                                                        in1=wts[s][:, n, :], op0=ALU.is_lt, op1=ALU.mult))
                    count()
                part = [parts[s][:, n, i * E:(i + 1) * E] for i in range(3)]
                first = chain.add(nc.vector.tensor_copy(part[0], wts[s][:, n, :]))
                if not u.capped:
                    count()
                chain.wait(first)
                link(nc.vector.tensor_tensor(rest[s][:, n, :], wts[s][:, n, :], part[0], ALU.subtract))
                link(nc.vector.tensor_copy(part[1], rest[s][:, n, :]))
                nc.vector.tensor_tensor(part[2], rest[s][:, n, :], part[1], ALU.subtract).then_inc(parts_ready, 1)

            for stage in (stats_x, norm_x):
                for u in first_units:
                    stage(u)
            tables()
            for u in first_units:
                exponents(u)
            stats_x(early)
            dve.wait_ge(gate_hi_ready, 1)
            nc.vector.tensor_tensor(gate_lo[:], gate_sb[:], gate_hi[:].bitcast(F32), ALU.subtract).then_inc(gate_ready, 1)
            norm_x(early)
            state_q(*first_units)
            for u in first_units:
                state_p(u)
            differences = exponents(early, clamped=False)
            mix(*first_units)
            chain.wait(differences)
            clamp(early, slice(0, 2))
            add_mixed(*first_units)
            for u in first_units:
                norm_h(u)
            state_q(early)
            for u in first_units:
                h_low(u)
            invert(early)
            largest(first_routed)
            state_p(early)
            choose(first_routed)
            weigh(first_routed)
            mix(early)

            def step(n, k):
                dve.wait_ge(w_turned, n + 1)
                dve.wait_ge(s_ready, n + 1)
                dve.wait_ge(t_ready, n + 1)
                nc.vector.tensor_tensor(t1_sb[:], w_ps[:], s_sb[:], ALU.mult).then_inc(t1_ready, 1)
                dve.wait_ge(t1_ready, n + 2)
                dve.wait_ge(u_ready, n + 1)
                dve.wait_ge(t_hi_ready, n + 1)
                dve.wait_ge(t_lo_ready, n + 1)
                nc.vector.tensor_tensor(t_sb[:], u_ps[:], t1_sb[:], ALU.mult).then_inc(t_ready, 1)

            def turn(half, it, front, back, routed, first_turn=False):
                beside = {0: [(stats_x, front), (h_low, back), (norm_x, front)],
                          1: [(largest, routed), (exponents, front)], 2: [(choose, routed), (state_q, front)],
                          3: [(invert, front), (state_p, front)], 4: [(mix, front), (weigh, routed)], 5: [(add_mixed, front), (norm_h, front)]}
                if first_turn:
                    beside[0] = [(add_mixed, early), (norm_h, early)] + beside[0]
                for k in range(TURN_STEPS):
                    step(it * TURN_STEPS + (half * STEPS + k), k)
                    for stage, u in beside.get(k, []):
                        if u:
                            stage(u)

            LINKS = 22
            def take_y(half):
                dve.wait_ge(down_done, (half + 1) * STEPS + 2)
                if half:
                    dve.wait_ge(y_turned, 2)
                for q in range(2):
                    cols = slice(q * NT * P, (q + 1) * NT * P)
                    nc.vector.tensor_copy(y_sb[:, 1, cols], y_ps[1][:, cols]).then_inc(y_copied[1], 1)

            def add_output(half):
                for q in range(2):
                    dve.wait_ge(y_turned, half * 2 + q + 1)
                    for t in range(NT):
                        y = out_ps[q][:, t * C:(t + 1) * C].rearrange("p (k c) -> p c k", k=KT)
                        rows = x1[:, half * HT + q * NT + t, :].rearrange("p (c k) -> p c k", k=KT)
                        last = nc.vector.tensor_tensor(rows, rows, y, ALU.add)
                    last.then_inc(out_ready, 1)

            turn(0, 0, later(3), later(2), later_routed(2), first_turn=True)
            with dve.Fori(0, TURNS - 2) as again:
                chain.enter(again, LINKS)
                turn(0, again + 1, later(again + 4), later(again + 3), later_routed(again + 3))
            chain.leave(TURNS - 2)
            turn(0, TURNS - 1, None, later(TURNS + 1), later_routed(TURNS + 1))
            take_y(0)
            turn(1, 0, None, None, None)
            add_output(0)
            with dve.Fori(1, TURNS) as it:
                turn(1, it, None, None, None)
            dve.wait_ge(t_hi_ready, 2 * STEPS + 1)
            dve.wait_ge(t_lo_ready, 2 * STEPS)
            dve.wait_ge(down_done, 2 * STEPS)
            nc.vector.tensor_tensor(t_lo[1][:], t_sb[:], t_hi[1][:].bitcast(F32), ALU.subtract).then_inc(t_lo_ready, 1)
            take_y(1)
            add_output(1)


_INS = ['x', 'ctx_2048', 'L0_xattn_w', 'L0_xattn_u', 'L0_ffn_gate_w', 'L0_ffn_w_gate', 'L0_ffn_w_up', 'L0_ffn_w_down']
_OUTS = [((16, 64, 256), 'float32')]


def kernel(**inputs):
    import numpy as _np
    import concourse.bacc as _bacc
    from concourse import mybir as _mybir
    from concourse.bass_utils import run_bass_kernel_spmd as _run

    nc = _bacc.Bacc("TRN2", target_bir_lowering=False, num_devices=1)
    arrays, args = {}, []
    for name in _INS:
        a = _np.ascontiguousarray(inputs[name])
        arrays[f"in_{name}_dram"] = a
        args.append(nc.dram_tensor(f"in_{name}_dram", a.shape, _mybir.dt.from_np(a.dtype), kind="ExternalInput").ap())
    for i, (shape, dtype) in enumerate(_OUTS):
        dt = _mybir.dt.from_np(_np.dtype(dtype))
        args.append(nc.dram_tensor(f"out_{i}_dram", shape, dt, kind="ExternalOutput").ap())
    program(nc, *args)
    r = _run(nc, [arrays], core_ids=[0])
    got = tuple(r.results[0][f"out_{i}_dram"] for i in range(len(_OUTS)))
    return got[0]
```
